# Optimizing a Trainium2 kernel written in Bass

```python
import numpy as np
import jax
import jax.numpy as jnp

def _softmax(x, axis=-1):
    return jax.nn.softmax(x, axis=axis)

def _gelu(x):
    return jax.nn.gelu(x, approximate=True)

def _silu(x):
    return jax.nn.silu(x)

def _sigmoid(x):
    return jax.nn.sigmoid(x)

def _layernorm(x, axis=-1, eps=1e-05):
    m = jnp.mean(x, axis=axis, keepdims=True)
    v = jnp.var(x, axis=axis, keepdims=True)
    return (x - m) / jnp.sqrt(v + eps)

def _scatter_add(tgt, idx, src, axis=0):
    return tgt.at[idx].add(src)

def _segment_sum(src, seg, n):
    return jax.ops.segment_sum(src, seg, n)
kernel_name = 'mk_macaron_d1_jaxref_r8_c2c39a'

def setup_inputs(seed: int=0):
    np.random.seed(seed)
    _w = jnp.asarray

    def _L0_attn_setup():
        import jax, jax.numpy as jnp
        import numpy as np
        from jax import lax
        D_MODEL, D_STATE, D_CONV, EXPAND = (128, 16, 4, 2)
        D_INNER = EXPAND * D_MODEL
        DT_RANK = (D_MODEL + 15) // 16
        B, T = (4, 256)

        def _causal_depthwise_conv(xb, conv_w, conv_b):
            inp = xb.transpose(0, 2, 1)
            ker = conv_w[:, None, :]
            dn = lax.conv_dimension_numbers(inp.shape, ker.shape, ('NCH', 'OIH', 'NCH'))
            out = lax.conv_general_dilated(inp, ker, window_strides=(1,), padding=[(D_CONV - 1, 0)], dimension_numbers=dn, feature_group_count=D_INNER)
            return (out + conv_b[None, :, None]).transpose(0, 2, 1)
        key = jax.random.key(seed)
        ks = jax.random.split(key, 10)
        s = lambda fan_in: 1.0 / np.sqrt(fan_in)
        return {'x': jax.random.normal(ks[0], (B, T, D_MODEL), dtype=jnp.float32), 'in_proj_w': jax.random.normal(ks[1], (D_MODEL, 2 * D_INNER), dtype=jnp.float32) * s(D_MODEL), 'conv_w': jax.random.normal(ks[2], (D_INNER, D_CONV), dtype=jnp.float32) * s(D_CONV), 'conv_b': jax.random.normal(ks[3], (D_INNER,), dtype=jnp.float32) * 0.1, 'x_proj_w': jax.random.normal(ks[4], (D_INNER, DT_RANK + 2 * D_STATE), dtype=jnp.float32) * s(D_INNER), 'dt_proj_w': jax.random.normal(ks[5], (DT_RANK, D_INNER), dtype=jnp.float32) * s(DT_RANK), 'dt_proj_b': jax.random.normal(ks[6], (D_INNER,), dtype=jnp.float32) * 0.1, 'A_log': jax.random.normal(ks[7], (D_INNER, D_STATE), dtype=jnp.float32) * 0.5, 'D_param': jnp.ones((D_INNER,), dtype=jnp.float32), 'out_proj_w': jax.random.normal(ks[8], (D_INNER, D_MODEL), dtype=jnp.float32) * s(D_INNER)}
    _L0_attn_in = _L0_attn_setup()

    def _L0_ffn_setup():
        import jax, jax.numpy as jnp
        import numpy as np
        B, S, D, E, K = (2, 256, 128, 8, 2)
        H = 4 * D
        key = jax.random.key(seed)
        ks = jax.random.split(key, 6)
        x = jax.random.normal(ks[0], (B, S, D), dtype=jnp.float32)
        lim_g = np.sqrt(6.0 / (D + E)).astype(np.float32)
        W_gate = jax.random.uniform(ks[1], (D, E), minval=-lim_g, maxval=lim_g, dtype=jnp.float32)
        lim1 = np.sqrt(1.0 / D).astype(np.float32)
        lim2 = np.sqrt(1.0 / H).astype(np.float32)
        W1 = jax.random.uniform(ks[2], (E, D, H), minval=-lim1, maxval=lim1, dtype=jnp.float32)
        b1 = jax.random.uniform(ks[3], (E, H), minval=-lim1, maxval=lim1, dtype=jnp.float32)
        W2 = jax.random.uniform(ks[4], (E, H, D), minval=-lim2, maxval=lim2, dtype=jnp.float32)
        b2 = jax.random.uniform(ks[5], (E, D), minval=-lim2, maxval=lim2, dtype=jnp.float32)
        return {'x': x, 'W_gate': W_gate, 'W1': W1, 'b1': b1, 'W2': W2, 'b2': b2}
    _L0_ffn_in = _L0_ffn_setup()
    _d = {'L0_attn_x': _L0_attn_in['x'], 'L0_attn_in_proj_w': _L0_attn_in['in_proj_w'], 'L0_attn_conv_w': _L0_attn_in['conv_w'], 'L0_attn_conv_b': _L0_attn_in['conv_b'], 'L0_attn_x_proj_w': _L0_attn_in['x_proj_w'], 'L0_attn_dt_proj_w': _L0_attn_in['dt_proj_w'], 'L0_attn_dt_proj_b': _L0_attn_in['dt_proj_b'], 'L0_attn_A_log': _L0_attn_in['A_log'], 'L0_attn_D_param': _L0_attn_in['D_param'], 'L0_attn_out_proj_w': _L0_attn_in['out_proj_w'], 'L0_ffn_W_gate': _L0_ffn_in['W_gate'], 'L0_ffn_W1': _L0_ffn_in['W1'], 'L0_ffn_b1': _L0_ffn_in['b1'], 'L0_ffn_W2': _L0_ffn_in['W2'], 'L0_ffn_b2': _L0_ffn_in['b2']}
    _x0 = _d['L0_attn_x']
    _d['L0_attn_x'] = jax.random.normal(jax.random.fold_in(jax.random.key(seed), 1), (4, 512, 128), dtype=_x0.dtype)
    del _x0
    return _d

def reference(L0_attn_x, L0_attn_in_proj_w, L0_attn_conv_w, L0_attn_conv_b, L0_attn_x_proj_w, L0_attn_dt_proj_w, L0_attn_dt_proj_b, L0_attn_A_log, L0_attn_D_param, L0_attn_out_proj_w, L0_ffn_W_gate, L0_ffn_W1, L0_ffn_b1, L0_ffn_W2, L0_ffn_b2):

    def _L0_attn_ref(x, in_proj_w, conv_w, conv_b, x_proj_w, dt_proj_w, dt_proj_b, A_log, D_param, out_proj_w):
        import jax, jax.numpy as jnp
        import numpy as np
        from jax import lax
        D_MODEL, D_STATE, D_CONV, EXPAND = (128, 16, 4, 2)
        D_INNER = EXPAND * D_MODEL
        DT_RANK = (D_MODEL + 15) // 16
        B, T = (4, 256)

        def _causal_depthwise_conv(xb, conv_w, conv_b):
            inp = xb.transpose(0, 2, 1)
            ker = conv_w[:, None, :]
            dn = lax.conv_dimension_numbers(inp.shape, ker.shape, ('NCH', 'OIH', 'NCH'))
            out = lax.conv_general_dilated(inp, ker, window_strides=(1,), padding=[(D_CONV - 1, 0)], dimension_numbers=dn, feature_group_count=D_INNER)
            return (out + conv_b[None, :, None]).transpose(0, 2, 1)
        xz = x @ in_proj_w
        xb, z = jnp.split(xz, 2, axis=-1)
        xb = jax.nn.silu(_causal_depthwise_conv(xb, conv_w, conv_b))
        proj = xb @ x_proj_w
        dt = jax.nn.softplus(proj[..., :DT_RANK] @ dt_proj_w + dt_proj_b)
        b = proj[..., DT_RANK:DT_RANK + D_STATE]
        c = proj[..., DT_RANK + D_STATE:]
        a = -jnp.exp(A_log)

        def step(state, ts):
            u_t, dt_t, b_t, c_t = ts
            da = jnp.exp(dt_t[:, :, None] * a)
            dbu = dt_t[:, :, None] * b_t[:, None, :] * u_t[:, :, None]
            state = da * state + dbu
            y_t = jnp.einsum('bds,bs->bd', state, c_t)
            return (state, y_t)
        state0 = jnp.zeros((x.shape[0], D_INNER, D_STATE), dtype=x.dtype)
        to_t = lambda v: jnp.swapaxes(v, 0, 1)
        _, ys = lax.scan(step, state0, (to_t(xb), to_t(dt), to_t(b), to_t(c)))
        y = jnp.swapaxes(ys, 0, 1)
        y = (y + D_param * xb) * jax.nn.silu(z)
        return y @ out_proj_w

    def _L0_ffn_ref(x, W_gate, W1, b1, W2, b2):
        import jax, jax.numpy as jnp
        import numpy as np
        B, S, D, E, K = (2, 256, 128, 8, 2)
        H = 4 * D
        gate = jnp.einsum('bsd,de->bse', x, W_gate)
        kth = jax.lax.top_k(gate, K)[0][..., -1:]
        mask = jax.nn.softmax(jnp.where(gate >= kth, gate, -jnp.inf), axis=-1)
        h = jax.nn.relu(jnp.einsum('bsd,edh->bseh', x, W1) + b1)
        y = jnp.einsum('bseh,ehd->bsed', h, W2) + b2
        return (y * mask[..., None]).mean(axis=-2)
    x = L0_attn_x
    x = x + 0.5 * _L0_ffn_ref(_layernorm(x, axis=-1), L0_ffn_W_gate, L0_ffn_W1, L0_ffn_b1, L0_ffn_W2, L0_ffn_b2)
    x = x + _L0_attn_ref(_layernorm(x, axis=-1), L0_attn_in_proj_w, L0_attn_conv_w, L0_attn_conv_b, L0_attn_x_proj_w, L0_attn_dt_proj_w, L0_attn_dt_proj_b, L0_attn_A_log, L0_attn_D_param, L0_attn_out_proj_w)
    x = x + 0.5 * _L0_ffn_ref(_layernorm(x, axis=-1), L0_ffn_W_gate, L0_ffn_W1, L0_ffn_b1, L0_ffn_W2, L0_ffn_b2)
    return x

_drawn_inputs = setup_inputs


def setup_inputs(seed=0):
    import zlib

    import numpy as np

    out = dict(_drawn_inputs(seed))
    spreads = {'L0_attn_D_param': (1.0, 0.2)}
    factors = {'L0_ffn_W_gate': 3.018, 'L0_ffn_W1': 3.243, 'L0_ffn_b1': 26.881, 'L0_ffn_b2': 8.0}
    for name, (base, spread) in spreads.items():
        noise = np.random.default_rng([zlib.crc32(name.encode()), seed]).standard_normal(out[name].shape)
        drawn = base * np.exp(spread * noise) if base else spread * noise
        out[name] = jnp.asarray(drawn.astype(out[name].dtype))
    for name, factor in factors.items():
        out[name] = (out[name] * factor).astype(out[name].dtype)
    return out
```

```python
from contextlib import ExitStack

import concourse.bass as bass
from concourse import mybir


def macaron_kernel(nc, x, in_proj_w, conv_w, conv_b, x_proj_w, dt_proj_w, dt_proj_b, A_log, D_param,
                   out_proj_w, W_gate, W1, b1, W2, b2, ident_in, out):
    f32, f32r = mybir.dt.float32, mybir.dt.float32r
    ALU, ACT, AX = mybir.AluOpType, mybir.ActivationFunctionType, mybir.AxisListType

    P = 128
    B, T, D = x.shape
    TT = T // P
    E, _, H = W1.shape
    HT = H // P
    UNITS = E * HT
    DI = conv_w.shape[0]
    NH = DI // P
    TAPS = conv_w.shape[1]
    S = A_log.shape[1]
    R = dt_proj_w.shape[0]
    EPS = 1e-5
    FFN_SCALE = 0.5 / E

    ctx = ExitStack()
    with ctx:
        def sb(name, shape, dt=f32):
            return ctx.enter_context(nc.sbuf_tensor(name, shape, dt))

        def sem(name):
            return ctx.enter_context(nc.semaphore(name))

        ident = sb("ident", [P, P])
        w1_stage = sb("w1_stage", [P, 2, H])
        w1_hi = sb("w1_hi", [P, E, H], f32r)
        w1_lo = sb("w1_lo", [P, E, H], f32r)
        w2 = sb("w2", [P, E, HT, D])
        VECS = UNITS + 3 * NH
        vec_rows = sb("vec_rows", [VECS, P])
        vec_cols = sb("vec_cols", [P, VECS])
        b2_sb = sb("b2_sb", [E, D])
        w_gate = sb("w_gate", [P, E])
        in_stage = sb("in_stage", [P, 2 * DI])
        in_hi = sb("in_hi", [P, 2 * DI], f32r)
        in_lo = sb("in_lo", [P, 2 * DI], f32r)
        conv_sb = sb("conv_sb", [P, NH, TAPS])
        conv_half = sb("conv_half", [P, NH, TAPS])
        convb_half = sb("convb_half", [P, NH])
        xproj_sb = sb("xproj_sb", [P, NH, 2 * S + R])
        dtw_sb = sb("dtw_sb", [2 * S + R, DI])
        alog_sb = sb("alog_sb", [P, NH, S])
        aexp_sb = sb("aexp_sb", [P, NH, S])
        a_neg = sb("a_neg", [P, NH, S])
        convb_sb, dtb_sb, dskip_sb = (vec_cols[:, UNITS + i * NH:UNITS + (i + 1) * NH] for i in range(3))
        outp_sb = sb("outp_sb", [P, NH, D])
        outp_half = sb("outp_half", [P, NH, D])
        spread = sb("spread", [4 * S, 2 * S, P], f32r)
        neg_half = sb("neg_half", [P, TT])

        xres = sb("xres", [P, B, TT, D])

        f_stat = sb("f_stat", [P, TT, 6])
        f_mv = sb("f_mv", [P, TT, 2])
        f_var = sb("f_var", [P, TT])
        f_rstd = sb("f_rstd", [P, TT])
        f_norm = sb("f_norm", [P, TT, D])
        f_xT = sb("f_xT", [P, T])
        f_xhi = sb("f_xhi", [P, T], f32r)
        f_xlo = sb("f_xlo", [P, T], f32r)
        gate = sb("gate", [P, TT, E])
        top = sb("top", [P, TT, 8])
        gshift = sb("gshift", [P, TT, E])
        gkeep = sb("gkeep", [P, TT, E])
        gexp = sb("gexp", [P, TT, E])
        gsum = sb("gsum", [P, TT])
        grec = sb("grec", [P, TT])
        mask = sb("mask", [P, TT, E])
        maskT = sb("maskT", [E, T])
        mask_bc = sb("mask_bc", [P, E, T])
        NHB = 4
        hid = sb("hid", [P, NHB, T])
        y_part = sb("y_part", [P, 2, T])
        y_sum = sb("y_sum", [P, T])

        m_stat = sb("m_stat", [P, TT, 6])
        m_mv = sb("m_mv", [P, TT, 2])
        m_var = sb("m_var", [P, TT])
        m_rstd = sb("m_rstd", [P, TT])
        m_norm = sb("m_norm", [P, TT, D])
        m_xhi = sb("m_xhi", [P, T], f32r)
        m_xlo = sb("m_xlo", [P, T], f32r)
        xpad = sb("xpad", [P, NH, TAPS - 1 + T])
        zg = sb("zg", [P, NH, T])
        u = sb("u", [P, NH, T])
        bc = sb("bc", [4 * S, T], f32r)
        dt_low = sb("dt_low", [2 * S + R, T])
        dt = sb("dt", [P, NH, T])
        dtu = sb("dtu", [P, NH, T])
        decay = sb("decay", [P, 2, NH, T])
        inject = sb("inject", [P, 2, NH, T])
        state = sb("state", [P, 2, NH, T])
        read = sb("read", [P, 2, NH, T])
        y_ssm = sb("y_ssm", [P, NH, T])
        conv, dt_abs = read[:, 0], read[:, 1]
        conv_th, z_th = state[:, 0], state[:, 1]
        dt_lin = inject[:, 1]

        mask_dram = nc.dram_tensor("mask_dram", (E, T), f32).ap()

        def pb(name):
            return ctx.enter_context(nc.psum_tensor(name, [P, T], f32))

        z_ps = [pb("z_ps0"), pb("z_ps1")]
        ye_ps = [pb("ye_ps0"), pb("ye_ps1")]
        fs_ps = pb("fs_ps")
        ms_ps = pb("ms_ps")
        b_ps = pb("b_ps")
        c_ps = pb("c_ps")

        ld_x = [sem(f"ld_x{b}") for b in range(B)]
        ld_w1 = [sem(f"ld_w1_{i}") for i in range(2)]
        ld_w2 = [sem(f"ld_w2_{i}") for i in range(4)]
        ld_small = sem("ld_small")
        ld_mix = sem("ld_mix")
        w1_hi_done = sem("w1_hi_done")
        w1_lo_done = sem("w1_lo_done")
        vec_turned = sem("vec_turned")
        vec_ready = sem("vec_ready")
        const_set = sem("const_set")
        spread_set = sem("spread_set")
        mix_prep = sem("mix_prep")
        mix_exp = sem("mix_exp")
        mix_split = sem("mix_split")
        x_written = sem("x_written")

        f_ln, f_pow = sem("f_ln"), sem("f_pow")
        f_turned, f_copied, f_lo = sem("f_turned"), sem("f_copied"), sem("f_lo")
        f_gated, f_route, f_exp = sem("f_gated"), sem("f_route"), sem("f_exp")
        f_mturned, f_mcopied = sem("f_mturned"), sem("f_mcopied")
        mask_out, mask_in = sem("mask_out"), sem("mask_in")
        f_up, f_relu, f_down = sem("f_up"), sem("f_relu"), sem("f_down")
        f_scaled, f_added, f_back = sem("f_scaled"), sem("f_added"), sem("f_back")

        m_ln, m_pow = sem("m_ln"), sem("m_pow")
        m_turned, m_hi, m_lo = sem("m_turned"), sem("m_hi"), sem("m_lo")
        m_inproj, m_evac, m_conv, m_tanh = sem("m_inproj"), sem("m_evac"), sem("m_conv"), sem("m_tanh")
        m_gz, m_u, m_xproj, m_bchi, m_bclo = sem("m_gz"), sem("m_u"), sem("m_xproj"), sem("m_bchi"), sem("m_bclo")
        m_dtproj, m_soft, m_dt, m_dtu = sem("m_dtproj"), sem("m_soft"), sem("m_dt"), sem("m_dtu")
        m_B, m_C, m_decay, m_inject = sem("m_B"), sem("m_C"), sem("m_decay"), sem("m_inject")
        m_scan, m_read, m_sum = sem("m_scan"), sem("m_read"), sem("m_sum")
        m_y, m_outproj = sem("m_y"), sem("m_outproj")
        stored = sem("stored")

        F_HEAD = ["ln", "turn", "gate", "route", "mask"]

        def pass_steps(n):
            return ([("F", s, n) for s in F_HEAD] + [("F", i, n) for i in range(UNITS)]
                    + [("F", "tail", n), ("F", "epi", n)])

        M_HEAD = ["ln", "turn", "inproj", "conv", "xproj", "dtproj", "soft"]
        M_STEPS = ([("M", s, 0) for s in M_HEAD] + [("M", s, 0) for s in range(S)]
                   + [("M", "gather", 0), ("M", "epi", 0)])

        def weave(passes):
            fs = [st for n in range(passes) for st in pass_steps(n)]
            steps, done = [], 0
            for j, m in enumerate(M_STEPS):
                steps.append(m)
                upto = (j + 1) * len(fs) // len(M_STEPS)
                steps += fs[done:upto]
                done = upto
            return steps

        EVEN, ODD = weave(1), weave(2)
        LOOP_PASSES = 3
        WRITES = {}
        n_w = 0
        for name, steps in (("even", EVEN), ("odd", ODD)):
            for st in steps:
                if st[1] == "ln":
                    WRITES[(name, st)] = n_w
                if st[1] == "epi":
                    n_w += 1
        assert n_w == LOOP_PASSES + 2

        def run(step_f, step_m, fori):
            for _, st, _ in pass_steps(0):
                step_f(st, 0, 0, 0)
            for k in range(2):
                for name, steps, g0, m0 in (("even", EVEN, 1, 0), ("odd", ODD, 2, 1)):
                    for st in steps:
                        w = 1 + n_w * k + WRITES[(name, st)] if st[1] == "ln" else None
                        if st[0] == "F":
                            n = g0 + st[2]
                            step_f(st[1], n + LOOP_PASSES * k, n - k, w)
                        else:
                            step_m(st[1], m0 + 2 * k, w)
            for _, st, _ in pass_steps(0):
                step_f(st, 2 * B - 1, B - 1, 1 + 2 * n_w)

        def part(eng):
            eng.wait_ge(ld_small, 112)

        def value(eng, v):
            return v if isinstance(v, int) else eng.snap(v)

        block = ctx.enter_context(nc.Block())

        @block.sync
        def _(sp):
            xv = x.rearrange("b (t p) d -> b p t d", p=P)
            ov = out.rearrange("b (t p) d -> b p t d", p=P)
            sp.dma_start(xres[:, 0, :, :], xv[0]).then_inc(ld_x[0], 16)
            sp.dma_start(ident[:, :], ident_in).then_inc(ld_small, 16)
            sp.dma_start(w_gate[:, :], W_gate).then_inc(ld_small, 16)
            sp.dma_start(vec_rows[0:UNITS, :], b1.rearrange("e (h p) -> (e h) p", p=P)).then_inc(ld_small, 16)
            for i, v in enumerate((conv_b, dt_proj_b, D_param)):
                sp.dma_start(vec_rows[UNITS + i * NH:UNITS + (i + 1) * NH, :],
                             v.rearrange("(h p) -> h p", p=P)).then_inc(ld_small, 16)
            sp.dma_start(b2_sb[:, :], b2).then_inc(ld_small, 16)
            for e in range(E):
                if e >= 2:
                    sp.wait_ge(w1_lo_done, e - 1)
                sp.dma_start(w1_stage[:, e % 2, :], W1[e]).then_inc(ld_w1[e % 2], 16)
                if e % 2 == 1:
                    sp.dma_start(w2[:, e - 1:e + 1, :, :],
                                 W2[e - 1:e + 1].rearrange("e (h p) d -> p e h d", p=P)).then_inc(ld_w2[e // 2], 16)
            for b in range(1, B):
                sp.dma_start(xres[:, b, :, :], xv[b]).then_inc(ld_x[b], 16)
            sp.dma_start(in_stage[:, :], in_proj_w).then_inc(ld_mix, 16)
            sp.dma_start(conv_sb[:, :, :], conv_w.rearrange("(h p) k -> p h k", p=P)).then_inc(ld_mix, 16)
            xpv = x_proj_w.rearrange("(h p) r -> p h r", p=P)
            sp.dma_start(xproj_sb[:, :, 0:2 * S], xpv[:, :, R:R + 2 * S]).then_inc(ld_mix, 16)
            sp.dma_start(xproj_sb[:, :, 2 * S:], xpv[:, :, 0:R]).then_inc(ld_mix, 16)
            sp.dma_start(dtw_sb[2 * S:, :], dt_proj_w).then_inc(ld_mix, 16)
            sp.dma_start(alog_sb[:, :, :], A_log.rearrange("(h p) s -> p h s", p=P)).then_inc(ld_mix, 16)
            sp.dma_start(outp_sb[:, :, :], out_proj_w.rearrange("(h p) d -> p h d", p=P)).then_inc(ld_mix, 16)

            def step_f(st, g, b, w):
                if st != "mask":
                    return
                v = value(sp, g + 1)
                part(sp)
                sp.wait_ge(f_mcopied, v)
                sp.dma_start(mask_dram, maskT[:, :]).then_inc(mask_out, 16)
                v = value(sp, 16 * g + 16)
                part(sp)
                sp.wait_ge(mask_out, v)
                if not (isinstance(g, int) and g == 0):
                    v = value(sp, E * g)
                    part(sp)
                    sp.wait_ge(f_scaled, v)
                sp.dma_start(mask_bc[:, :, :].rearrange("p e t -> p (e t)"),
                             mask_dram.rearrange("e t -> (e t)").partition_broadcast(P)).then_inc(mask_in, 16)

            run(step_f, lambda *_: None, sp.Fori)
            for b in range(B):
                sp.wait_ge(x_written, 2 + 2 * n_w)
                sp.dma_start(ov[b], xres[:, b, :, :]).then_inc(stored, 16)
            sp.wait_ge(stored, 16 * B)

        @block.gpsimd
        def _(pool):
            nc.gpsimd.memset(neg_half[:, :], -0.5).then_inc(const_set, 1)
            nc.gpsimd.memset(xpad[:, :, 0:TAPS - 1], 0.0).then_inc(const_set, 1)
            pool.wait_ge(ld_small, 112)
            pool.wait_ge(const_set, 2)
            for r in (0, 2 * S):
                if r:
                    pool.wait_ge(spread_set, 1)
                src = ident[r:r + 2 * S, r:r + 2 * S].unsqueeze(2).to_broadcast([2 * S, 2 * S, P])
                nc.gpsimd.tensor_copy(spread[r:r + 2 * S, :, :], src).then_inc(spread_set, 1)
            pool.wait_ge(spread_set, 2)

            def step_f(st, g, b, w):
                if st == "ln":
                    pool.wait_ge(f_ln, 4 * g + 3)
                    nc.gpsimd.tensor_tensor(f_rstd[:, :], f_var[:, :], neg_half[:, :], ALU.pow).then_inc(f_pow, 1)
                if isinstance(st, int) and st % HT == 3 and st // HT >= 2:
                    add(g, st // HT - 1)
                if st == "tail":
                    add(g, E - 1)

            def add(g, e):
                pool.wait_ge(f_scaled, E * g + e + 1)
                if e >= 2:
                    pool.wait_ge(f_added, (E - 1) * g + e - 1)
                nc.gpsimd.tensor_tensor(y_sum[:, :], y_sum[:, :], y_part[:, e % 2, :], ALU.add).then_inc(f_added, 1)

            def step_m(st, m, w):
                if st == "ln":
                    pool.wait_ge(m_ln, 4 * m + 3)
                    nc.gpsimd.tensor_tensor(m_rstd[:, :], m_var[:, :], neg_half[:, :], ALU.pow).then_inc(m_pow, 1)
                if isinstance(st, int) and st >= 1:
                    pool.wait_ge(m_read, S * m + st + 1)
                    if st >= 2:
                        pool.wait_ge(m_sum, (S - 1) * m + st - 1)
                    nc.gpsimd.tensor_tensor(y_ssm[:, :, :], y_ssm[:, :, :], read[:, st % 2, :, :], ALU.add)\
                        .then_inc(m_sum, 1)

            run(step_f, step_m, pool.Fori)

        @block.scalar
        def _(act):
            for e in range(E):
                act.wait_ge(ld_w1[e % 2], 16 * (e // 2 + 1))
                nc.scalar.copy(w1_hi[:, e, :], w1_stage[:, e % 2, :]).then_inc(w1_hi_done, 1)
                if e == 0:
                    act.wait_ge(vec_turned, 1)
                    nc.scalar.copy(vec_cols[:, :], fs_ps[:, 0:VECS]).then_inc(vec_ready, 1)
            act.wait_ge(ld_mix, 112)
            nc.scalar.copy(in_hi[:, :], in_stage[:, :]).then_inc(mix_exp, 1)
            nc.scalar.activation(aexp_sb[:, :, :], alog_sb[:, :, :], ACT.Exp).then_inc(mix_exp, 1)

            def step_f(st, g, b, w):
                if st == "turn":
                    act.wait_ge(f_turned, g + 1)
                    nc.scalar.copy(f_xT[:, :], fs_ps[:, :]).then_inc(f_copied, 1)
                    nc.scalar.copy(f_xhi[:, :], fs_ps[:, :]).then_inc(f_copied, 1)
                if st == "route":
                    act.wait_ge(f_route, 8 * g + 3)
                    nc.scalar.activation(gexp[:, :, :], gshift[:, :, :], ACT.Exp).then_inc(f_exp, 1)
                if st == "mask":
                    act.wait_ge(f_mturned, g + 1)
                    nc.scalar.copy(maskT[:, :], fs_ps[0:E, :]).then_inc(f_mcopied, 1)
                if isinstance(st, int):
                    act.wait_ge(f_up, UNITS * g + st + 1)
                    if not (isinstance(g, int) and g == 0 and st < NHB):
                        act.wait_ge(f_down, UNITS * g + st - NHB + 1)
                    nc.scalar.activation(hid[:, st % NHB, :], z_ps[st % 2][:, :], ACT.Relu,
                                         bias=vec_cols[:, st:st + 1]).then_inc(f_relu, 1)

            def decays(m, s):
                if s == 0:
                    act.wait_ge(m_dt, m + 1)
                if not (isinstance(m, int) and m == 0 and s < 2):
                    if s >= 2:
                        act.wait_ge(m_scan, NH * (S * m + s - 1))
                for h in range(NH):
                    nc.scalar.activation(decay[:, s % 2, h, :], dt[:, h, :], ACT.Exp,
                                         scale=a_neg[:, h, s:s + 1]).then_inc(m_decay, 1)

            def step_m(st, m, w):
                if st == "turn":
                    act.wait_ge(m_turned, m + 1)
                    nc.scalar.copy(m_xhi[:, :], ms_ps[:, :]).then_inc(m_hi, 1)
                if st == "inproj":
                    for j in range(2 * NH):
                        ps = (b_ps, c_ps, ms_ps, b_ps)[j]
                        act.wait_ge(m_inproj, 2 * NH * m + j + 1)
                        if j < NH:
                            nc.scalar.copy(xpad[:, j, TAPS - 1:], ps[:, :]).then_inc(m_evac, 1)
                        else:
                            nc.scalar.copy(zg[:, j - NH, :], ps[:, :])
                            nc.scalar.activation(z_th[:, j - NH, :], ps[:, :], ACT.Tanh, scale=0.5)\
                                .then_inc(m_evac, 1)
                if st == "conv":
                    act.wait_ge(m_conv, NH * TAPS * m + NH * TAPS)
                    nc.scalar.activation(conv_th[:, :, :], conv[:, :, :], ACT.Tanh).then_inc(m_tanh, 1)
                if st == "xproj":
                    act.wait_ge(m_xproj, m + 1)
                    nc.scalar.copy(bc[0:2 * S, :], ms_ps[0:2 * S, :]).then_inc(m_bchi, 1)
                    nc.scalar.copy(dt_low[2 * S:, :], ms_ps[2 * S:2 * S + R, :]).then_inc(m_bchi, 1)
                if st == "dtproj":
                    for h, ps in enumerate((b_ps, c_ps)):
                        act.wait_ge(m_dtproj, NH * m + h + 1)
                        nc.scalar.activation(dt_lin[:, h, :], ps[:, :], ACT.Identity, bias=dtb_sb[:, h:h + 1])
                        nc.scalar.activation(dt_abs[:, h, :], ps[:, :], ACT.Abs, bias=dtb_sb[:, h:h + 1])\
                            .then_inc(m_soft, 1)
                    act.wait_ge(m_soft, 4 * m + 2)
                    nc.scalar.activation(dt_abs[:, :, :], dt_abs[:, :, :], ACT.Exp, scale=-1.0).then_inc(m_soft, 1)
                    act.wait_ge(m_soft, 4 * m + 3)
                    nc.scalar.activation(dt_abs[:, :, :], dt_abs[:, :, :], ACT.Ln, bias=1.0).then_inc(m_soft, 1)
                if st == "soft":
                    decays(m, 0)
                if isinstance(st, int) and st + 1 < S:
                    decays(m, st + 1)

            run(step_f, step_m, act.Fori)

        @block.tensor
        def _(pe):
            pe.wait_ge(ld_small, 112)
            nc.tensor.transpose(fs_ps[:, 0:VECS], vec_rows[:, :], ident[0:VECS, 0:VECS]).then_inc(vec_turned, 1)
            pe.wait_ge(vec_ready, 1)

            def down(g, i):
                e, ht = i // HT, i % HT
                pe.wait_ge(f_relu, UNITS * g + i + 1)
                if ht == 0 and not (isinstance(g, int) and g == 0 and e < 2):
                    pe.wait_ge(f_scaled, E * g + e - 1)
                if isinstance(g, int) and g == 0 and ht == 0 and e % 2 == 0:
                    pe.wait_ge(ld_w2[e // 2], 16)
                nc.tensor.matmul(ye_ps[e % 2][:, :], w2[:, e, ht, :], hid[:, i % NHB, :],
                                 start=(ht == 0), stop=(ht == HT - 1)).then_inc(f_down, 1)

            def step_f(st, g, b, w):
                if st == "turn":
                    pe.wait_ge(f_ln, 4 * g + 4)
                    for t in range(TT):
                        mm = nc.tensor.transpose(fs_ps[:, t * P:(t + 1) * P], f_norm[:, t, :], ident[:, :])
                    mm.then_inc(f_turned, 1)
                if st == "gate":
                    pe.wait_ge(f_copied, 2 * g + 2)
                    for t in range(TT):
                        mm = nc.tensor.matmul(fs_ps[:, t * E:(t + 1) * E], f_xT[:, t * P:(t + 1) * P], w_gate[:, :],
                                              start=True, stop=True)
                    mm.then_inc(f_gated, 1)
                if st == "mask":
                    pe.wait_ge(f_route, 8 * g + 8)
                    for t in range(TT):
                        mm = nc.tensor.transpose(fs_ps[0:E, t * P:(t + 1) * P], mask[:, t, :], ident[:, :])
                    mm.then_inc(f_mturned, 1)
                if isinstance(st, int):
                    e = st // HT
                    if st == 0:
                        pe.wait_ge(f_lo, g + 1)
                    if isinstance(g, int) and g == 0 and st % HT == 0:
                        pe.wait_ge(w1_lo_done, e + 1)
                    if not (isinstance(g, int) and g == 0 and st < 2):
                        pe.wait_ge(f_relu, UNITS * g + st - 1)
                    cols = slice((st % HT) * P, (st % HT + 1) * P)
                    for i, (w, v) in enumerate(((w1_hi, f_xhi), (w1_hi, f_xlo), (w1_lo, f_xhi))):
                        mm = nc.tensor.matmul(z_ps[st % 2][:, :], w[:, e, cols], v[:, :], start=(i == 0), stop=(i == 2))
                    mm.then_inc(f_up, 1)
                    if st >= 2:
                        down(g, st - 2)
                if st == "tail":
                    down(g, UNITS - 2)
                    down(g, UNITS - 1)
                if st == "epi":
                    pe.wait_ge(f_added, (E - 1) * g + E - 1)
                    pe.wait_ge(f_mcopied, g + 1)
                    for t in range(TT):
                        cols = slice(t * P, (t + 1) * P)
                        nc.tensor.matmul(fs_ps[:, cols], y_sum[:, cols], ident[:, :], start=True, stop=False)
                        mm = nc.tensor.matmul(fs_ps[:, cols], maskT[:, cols], b2_sb[:, :], start=False, stop=True)
                    mm.then_inc(f_back, 1)

            def spread_row(ps, j):
                return nc.tensor.matmul(ps[:, :], spread[:, j, :], bc[:, :], start=True, stop=True)

            def step_m(st, m, w):
                if st == "turn":
                    pe.wait_ge(m_ln, 4 * m + 4)
                    for t in range(TT):
                        mm = nc.tensor.transpose(ms_ps[:, t * P:(t + 1) * P], m_norm[:, t, :], ident[:, :])
                    mm.then_inc(m_turned, 1)
                if st == "inproj":
                    pe.wait_ge(m_lo, m + 1)
                    pe.wait_ge(mix_split, 1)
                    for j in range(2 * NH):
                        ps = (b_ps, c_ps, ms_ps, b_ps)[j]
                        if j == 3:
                            pe.wait_ge(m_evac, 2 * NH * m + 1)
                        cols = slice(j * P, (j + 1) * P)
                        for i, (w_, v) in enumerate(((in_hi, m_xhi), (in_hi, m_xlo), (in_lo, m_xhi))):
                            mm = nc.tensor.matmul(ps[:, :], w_[:, cols], v[:, :], start=(i == 0), stop=(i == 2))
                        mm.then_inc(m_inproj, 1)
                if st == "xproj":
                    pe.wait_ge(m_u, m + 1)
                    pe.wait_ge(m_evac, 2 * NH * m + 4)
                    for h in range(NH):
                        mm = nc.tensor.matmul(ms_ps[0:2 * S + R, :], xproj_sb[:, h, :], u[:, h, :],
                                              start=(h == 0), stop=(h == NH - 1))
                    mm.then_inc(m_xproj, 1)
                if st == "dtproj":
                    pe.wait_ge(m_bchi, 2 * m + 2)
                    for h, ps in enumerate((b_ps, c_ps)):
                        nc.tensor.matmul(ps[:, :], dtw_sb[2 * S:, h * P:(h + 1) * P], dt_low[2 * S:, :],
                                         start=True, stop=True).then_inc(m_dtproj, 1)
                if st == "soft":
                    pe.wait_ge(m_bclo, m + 1)
                    pe.wait_ge(m_soft, 4 * m + 2)
                    pe.wait_ge(spread_set, 2)
                    spread_row(b_ps, 0).then_inc(m_B, 1)
                if isinstance(st, int):
                    if st >= 1:
                        pe.wait_ge(m_read, S * m + st)
                    spread_row(c_ps, S + st).then_inc(m_C, 1)
                    if st + 1 < S:
                        pe.wait_ge(m_inject, S * m + st + 1)
                        spread_row(b_ps, st + 1).then_inc(m_B, 1)
                if st == "epi":
                    pe.wait_ge(m_y, 3 * m + 3)
                    for t in range(TT):
                        cols = slice(t * P, (t + 1) * P)
                        for h in range(NH):
                            mm = nc.tensor.matmul(ms_ps[:, cols], y_ssm[:, h, cols], outp_half[:, h, :],
                                                  start=(h == 0), stop=(h == NH - 1))
                    mm.then_inc(m_outproj, 1)

            run(step_f, step_m, pe.Fori)

        @block.vector
        def _(dve):
            for e in range(E):
                dve.wait_ge(w1_hi_done, e + 1)
                nc.vector.tensor_tensor(w1_lo[:, e, :], w1_stage[:, e % 2, :], w1_hi[:, e, :].bitcast(f32), ALU.subtract)\
                    .then_inc(w1_lo_done, 1)
            dve.wait_ge(mix_exp, 2)
            nc.vector.tensor_tensor(in_lo[:, :], in_stage[:, :], in_hi[:, :].bitcast(f32), ALU.subtract).then_inc(mix_split, 1)
            nc.vector.tensor_scalar(a_neg[:, :, :], aexp_sb[:, :, :], -1.0, None, ALU.mult).then_inc(mix_prep, 1)
            nc.vector.tensor_scalar(conv_half[:, :, :], conv_sb[:, :, :], 0.5, None, ALU.mult).then_inc(mix_prep, 1)
            nc.vector.tensor_scalar(convb_half[:, :], convb_sb[:, :], 0.5, None, ALU.mult).then_inc(mix_prep, 1)
            nc.vector.tensor_scalar(outp_half[:, :, :], outp_sb[:, :, :], 0.5, None, ALU.mult).then_inc(mix_prep, 1)
            dve.wait_ge(mix_prep, 4)

            def layer_norm(src, stat, mv, var, rstd, norm, ln, power, n):
                for t in range(TT):
                    ins = nc.vector.bn_stats(stat[:, t, :], src(t))
                ins.then_inc(ln, 1)
                v = value(dve, 4 * n + 1)
                part(dve)
                dve.wait_ge(ln, v)
                for t in range(TT):
                    ins = nc.vector.bn_aggr(mv[:, t, :], stat[:, t, :])
                ins.then_inc(ln, 1)
                dve.wait_ge(ln, 4 * n + 2)
                nc.vector.tensor_scalar(var[:, :], mv[:, :, 1], EPS, None, ALU.add).then_inc(ln, 1)
                v = value(dve, n + 1)
                part(dve)
                dve.wait_ge(power, v)
                for t in range(TT):
                    ins = nc.vector.tensor_scalar(norm[:, t, :], src(t), mv[:, t, 0:1], rstd[:, t:t + 1],
                                                  ALU.subtract, ALU.mult)
                ins.then_inc(ln, 1)

            def per_token(v, j):
                return v[:, :, j:j + 1].to_broadcast([P, TT, E])

            def scale(g, e):
                dve.wait_ge(f_down, UNITS * g + HT * (e + 1))
                if e == 0:
                    dve.wait_ge(mask_in, 16 * g + 16)
                if e >= 3:
                    dve.wait_ge(f_added, (E - 1) * g + e - 2)
                dst = y_sum[:, :] if e == 0 else y_part[:, e % 2, :]
                nc.vector.tensor_tensor(dst, ye_ps[e % 2][:, :], mask_bc[:, e, :], ALU.mult).then_inc(f_scaled, 1)

            def step_f(st, g, b, w):
                if st == "ln":
                    if isinstance(g, int) and g == 0:
                        dve.wait_ge(ld_x[0], 16)
                    else:
                        for s_ in ld_x[1:]:
                            dve.wait_ge(s_, 16)
                        v = value(dve, w)
                        part(dve)
                        dve.wait_ge(x_written, v)
                    layer_norm(lambda t: xres[:, b, t, :], f_stat, f_mv, f_var, f_rstd, f_norm, f_ln, f_pow, g)
                if st == "turn":
                    dve.wait_ge(f_copied, 2 * g + 2)
                    nc.vector.tensor_tensor(f_xlo[:, :], f_xT[:, :], f_xhi[:, :].bitcast(f32), ALU.subtract)\
                        .then_inc(f_lo, 1)
                if st == "route":
                    r = 8 * g
                    dve.wait_ge(f_gated, g + 1)
                    nc.vector.tensor_copy(gate[:, :, :], fs_ps[:, 0:TT * E].rearrange("p (t e) -> p t e", e=E))\
                        .then_inc(f_route, 1)
                    v = value(dve, r + 1)
                    part(dve)
                    dve.wait_ge(f_route, v)
                    for t in range(TT):
                        ins = nc.vector.max(top[:, t, :], gate[:, t, :])
                    ins.then_inc(f_route, 1)
                    dve.wait_ge(f_route, r + 2)
                    nc.vector.tensor_tensor(gshift[:, :, :], gate[:, :, :], per_token(top, 0), ALU.subtract).then_inc(f_route, 1)
                    nc.vector.tensor_tensor(gkeep[:, :, :], gate[:, :, :], per_token(top, 1), ALU.is_ge).then_inc(f_route, 1)
                    dve.wait_ge(f_route, r + 4)
                    dve.wait_ge(f_exp, g + 1)
                    nc.vector.tensor_tensor(gexp[:, :, :], gexp[:, :, :], gkeep[:, :, :], ALU.mult).then_inc(f_route, 1)
                    dve.wait_ge(f_route, r + 5)
                    nc.vector.tensor_reduce(gsum[:, :], gexp[:, :, :], AX.X, ALU.add).then_inc(f_route, 1)
                    dve.wait_ge(f_route, r + 6)
                    nc.vector.reciprocal(grec[:, :], gsum[:, :]).then_inc(f_route, 1)
                    dve.wait_ge(f_route, r + 7)
                    nc.vector.scalar_tensor_tensor(out=mask[:, :, :], in0=gexp[:, :, :], scalar=FFN_SCALE,
                                                   in1=grec[:, :].unsqueeze(2).to_broadcast([P, TT, E]),
                                                   op0=ALU.mult, op1=ALU.mult).then_inc(f_route, 1)
                if isinstance(st, int) and st % HT == 2 and st // HT >= 1:
                    scale(g, st // HT - 1)
                if st == "tail":
                    scale(g, E - 1)
                if st == "epi":
                    v = value(dve, g + 1)
                    part(dve)
                    dve.wait_ge(f_back, v)
                    xb = xres[:, b, :, :].rearrange("p t d -> p (t d)")
                    nc.vector.tensor_tensor(xb, fs_ps[:, :], xb, ALU.add).then_inc(x_written, 1)

            def halves(ps):
                return ps[:, :].unsqueeze(1).to_broadcast([P, NH, T])

            def inject_step(m, s):
                dve.wait_ge(m_B, S * m + s + 1)
                nc.vector.tensor_tensor(inject[:, s % 2, :, :], dtu[:, :, :], halves(b_ps), ALU.mult).then_inc(m_inject, 1)

            def step_m(st, m, w):
                if st == "ln":
                    v = value(dve, w)
                    part(dve)
                    dve.wait_ge(x_written, v)
                    layer_norm(lambda t: xres[:, m, t, :], m_stat, m_mv, m_var, m_rstd, m_norm, m_ln, m_pow, m)
                if st == "turn":
                    dve.wait_ge(m_hi, m + 1)
                    nc.vector.tensor_tensor(m_xlo[:, :], ms_ps[:, :], m_xhi[:, :].bitcast(f32), ALU.subtract)\
                        .then_inc(m_lo, 1)
                if st == "conv":
                    dve.wait_ge(m_evac, 2 * NH * m + NH)
                    dve.wait_ge(const_set, 2)
                    for k in range(TAPS):
                        for h in range(NH):
                            n = NH * k + h
                            if k == 0:
                                ins = nc.vector.tensor_scalar(conv[:, h, :], xpad[:, h, 0:T], conv_half[:, h, 0:1],
                                                              convb_half[:, h:h + 1], ALU.mult, ALU.add)
                            else:
                                dve.wait_ge(m_conv, NH * TAPS * m + n - 1)
                                ins = nc.vector.scalar_tensor_tensor(
                                    out=conv[:, h, :], in0=xpad[:, h, k:k + T], scalar=conv_half[:, h, k:k + 1],
                                    in1=conv[:, h, :], op0=ALU.mult, op1=ALU.add)
                            ins.then_inc(m_conv, 1)
                    dve.wait_ge(m_evac, 2 * NH * m + 2 * NH)
                    nc.vector.scalar_tensor_tensor(out=zg[:, :, :], in0=z_th[:, :, :], scalar=1.0, in1=zg[:, :, :],
                                                   op0=ALU.add, op1=ALU.mult).then_inc(m_gz, 1)
                    dve.wait_ge(m_tanh, m + 1)
                    nc.vector.scalar_tensor_tensor(out=u[:, :, :], in0=conv_th[:, :, :], scalar=1.0, in1=conv[:, :, :],
                                                   op0=ALU.add, op1=ALU.mult).then_inc(m_u, 1)
                if st == "xproj":
                    dve.wait_ge(m_bchi, 2 * m + 1)
                    nc.vector.tensor_tensor(bc[2 * S:4 * S, :], ms_ps[0:2 * S, :], bc[0:2 * S, :].bitcast(f32), ALU.subtract)\
                        .then_inc(m_bclo, 1)
                if st == "soft":
                    dve.wait_ge(m_soft, 4 * m + 4)
                    nc.vector.scalar_tensor_tensor(out=dt[:, :, :], in0=dt_lin[:, :, :], scalar=0.0, in1=dt_abs[:, :, :],
                                                   op0=ALU.max, op1=ALU.add).then_inc(m_dt, 1)
                    dve.wait_ge(m_dt, m + 1)
                    dve.wait_ge(m_u, m + 1)
                    nc.vector.tensor_tensor(dtu[:, :, :], dt[:, :, :], u[:, :, :], ALU.mult).then_inc(m_dtu, 1)
                    dve.wait_ge(m_dtu, m + 1)
                    inject_step(m, 0)
                if isinstance(st, int):
                    n = S * m + st
                    dve.wait_ge(m_inject, n + 1)
                    for h in range(NH):
                        dve.wait_ge(m_decay, NH * n + h + 1)
                        nc.vector.tensor_tensor_scan(state[:, st % 2, h, :], decay[:, st % 2, h, :],
                                                     inject[:, st % 2, h, :], 0.0, ALU.mult, ALU.add).then_inc(m_scan, 1)
                    if st + 1 < S:
                        inject_step(m, st + 1)
                    dve.wait_ge(m_scan, NH * n + NH)
                    dve.wait_ge(m_C, n + 1)
                    if st >= 3:
                        dve.wait_ge(m_sum, (S - 1) * m + st - 2)
                    dst = y_ssm[:, :, :] if st == 0 else read[:, st % 2, :, :]
                    nc.vector.tensor_tensor(dst, state[:, st % 2, :, :], halves(c_ps), ALU.mult).then_inc(m_read, 1)
                if st == "gather":
                    dve.wait_ge(m_sum, (S - 1) * m + S - 1)
                    for h in range(NH):
                        ins = nc.vector.scalar_tensor_tensor(out=y_ssm[:, h, :], in0=u[:, h, :], scalar=dskip_sb[:, h:h + 1],
                                                             in1=y_ssm[:, h, :], op0=ALU.mult, op1=ALU.add)
                        ins.then_inc(m_y, 1)
                    dve.wait_ge(m_y, 3 * m + 2)
                    dve.wait_ge(m_gz, m + 1)
                    nc.vector.tensor_tensor(y_ssm[:, :, :], y_ssm[:, :, :], zg[:, :, :], ALU.mult).then_inc(m_y, 1)
                if st == "epi":
                    v = value(dve, m + 1)
                    part(dve)
                    dve.wait_ge(m_outproj, v)
                    xb = xres[:, m, :, :].rearrange("p t d -> p (t d)")
                    nc.vector.tensor_tensor(xb, ms_ps[:, :], xb, ALU.add).then_inc(x_written, 1)

            run(step_f, step_m, dve.Fori)


_INS = ["L0_attn_x", "L0_attn_in_proj_w", "L0_attn_conv_w", "L0_attn_conv_b", "L0_attn_x_proj_w",
        "L0_attn_dt_proj_w", "L0_attn_dt_proj_b", "L0_attn_A_log", "L0_attn_D_param", "L0_attn_out_proj_w",
        "L0_ffn_W_gate", "L0_ffn_W1", "L0_ffn_b1", "L0_ffn_W2", "L0_ffn_b2"]


def kernel(**inputs):
    import numpy as _np
    import concourse.bacc as _bacc
    from concourse import mybir as _mybir
    from concourse.bass_utils import run_bass_kernel_spmd as _run

    nc = _bacc.Bacc("TRN2", target_bir_lowering=False, num_devices=1)
    arrays, args = {}, []
    for name in _INS:
        a = _np.ascontiguousarray(inputs[name])
        arrays[f"in_{name}_dram"] = a
        args.append(nc.dram_tensor(f"in_{name}_dram", a.shape, _mybir.dt.from_np(a.dtype), kind="ExternalInput").ap())
    ident = _np.eye(128, dtype=_np.float32)
    arrays["in_ident_dram"] = ident
    args.append(nc.dram_tensor("in_ident_dram", ident.shape, _mybir.dt.float32, kind="ExternalInput").ap())
    shape = tuple(inputs["L0_attn_x"].shape)
    args.append(nc.dram_tensor("out_0_dram", shape, _mybir.dt.float32, kind="ExternalOutput").ap())
    macaron_kernel(nc, *args)
    r = _run(nc, [arrays], core_ids=[0])
    return r.results[0]["out_0_dram"]
```

```python
from contextlib import ExitStack

import concourse.bass as bass
from concourse import mybir


def macaron_kernel(nc, x, in_proj_w, conv_w, conv_b, x_proj_w, dt_proj_w, dt_proj_b, A_log, D_param,
                   out_proj_w, W_gate, W1, b1, W2, b2, ident_in, out):
    f32, f32r = mybir.dt.float32, mybir.dt.float32r
    ALU, ACT, AX = mybir.AluOpType, mybir.ActivationFunctionType, mybir.AxisListType

    P = 128
    B, T, D = x.shape
    TT = T // P
    E, _, H = W1.shape
    HT = H // P
    UNITS = E * HT
    DI = conv_w.shape[0]
    NH = DI // P
    TAPS = conv_w.shape[1]
    S = A_log.shape[1]
    R = dt_proj_w.shape[0]
    EPS = 1e-5
    FFN_SCALE = 0.5 / E

    ctx = ExitStack()
    with ctx:
        def sb(name, shape, dt=f32):
            return ctx.enter_context(nc.sbuf_tensor(name, shape, dt))

        def sem(name):
            return ctx.enter_context(nc.semaphore(name))

        ident = sb("ident", [P, P])
        w1_hi = sb("w1_hi", [P, E, H], f32r)
        w1_lo = sb("w1_lo", [P, E, H], f32r)
        w2 = sb("w2", [P, E, HT, D])
        VECS = UNITS + 3 * NH
        vec_rows = sb("vec_rows", [VECS, P])
        vec_cols = sb("vec_cols", [P, VECS])
        b2_sb = sb("b2_sb", [E, D])
        w_gate = sb("w_gate", [P, E])
        in_hi = sb("in_hi", [P, 2 * DI], f32r)
        in_lo = sb("in_lo", [P, 2 * DI], f32r)
        conv_sb = sb("conv_sb", [P, NH, TAPS])
        conv_half = sb("conv_half", [P, NH, TAPS])
        convb_half = sb("convb_half", [P, NH])
        xproj_sb = sb("xproj_sb", [P, NH, 2 * S + R])
        dtw_sb = sb("dtw_sb", [2 * S + R, DI])
        alog_sb = sb("alog_sb", [P, NH, S])
        aexp_sb = sb("aexp_sb", [P, NH, S])
        a_neg = sb("a_neg", [P, NH, S])
        convb_sb, dtb_sb, dskip_sb = (vec_cols[:, UNITS + i * NH:UNITS + (i + 1) * NH] for i in range(3))
        outp_sb = sb("outp_sb", [P, NH, D])
        outp_half = sb("outp_half", [P, NH, D])
        spread = sb("spread", [4 * S, 2 * S, P], f32r)
        neg_half = sb("neg_half", [P, TT])
        unused = sb("unused", [P, 1])

        xres = sb("xres", [P, B, TT, D])

        f_stat = sb("f_stat", [P, TT, 6])
        f_mv = sb("f_mv", [P, TT, 2])
        f_var = sb("f_var", [P, TT])
        f_rstd = sb("f_rstd", [P, TT])
        f_norm = sb("f_norm", [P, TT, D])
        f_xT = sb("f_xT", [P, T])
        f_xhi = sb("f_xhi", [P, T], f32r)
        f_xlo = sb("f_xlo", [P, T], f32r)
        gate = sb("gate", [P, TT, E])
        top = sb("top", [P, TT, 8])
        gshift = sb("gshift", [P, TT, E])
        gkeep = sb("gkeep", [P, TT, E])
        gexp = sb("gexp", [P, TT, E])
        gsum = sb("gsum", [P, TT])
        grec = sb("grec", [P, TT])
        mask = sb("mask", [P, TT, E])
        maskT = sb("maskT", [E, T])
        mask_bc = sb("mask_bc", [P, E, T])
        NHB = 4
        hid = sb("hid", [P, NHB, T])
        y_part = sb("y_part", [P, 2, T])
        y_sum = sb("y_sum", [P, T])

        m_stat = sb("m_stat", [P, TT, 6])
        m_mv = sb("m_mv", [P, TT, 2])
        m_var = sb("m_var", [P, TT])
        m_rstd = sb("m_rstd", [P, TT])
        m_xhi = sb("m_xhi", [P, T], f32r)
        m_xlo = sb("m_xlo", [P, T], f32r)
        xpad = sb("xpad", [P, NH, TAPS - 1 + T])
        zg = sb("zg", [P, 2, NH, T])
        u = sb("u", [P, 2, NH, T])
        conv = sb("conv", [P, NH, T])
        conv_th = sb("conv_th", [P, NH, T])
        bc = sb("bc", [4 * S, T], f32r)
        dt_low = sb("dt_low", [2 * S + R, T])
        dt = sb("dt", [P, NH, T])
        dtu = sb("dtu", [P, NH, T])
        decay = sb("decay", [P, 2, NH, T])
        inject = sb("inject", [P, 2, NH, T])
        state = sb("state", [P, 2, NH, T])
        read = sb("read", [P, 2, NH, T])
        y_ssm = sb("y_ssm", [P, NH, T])
        z_th, dt_lin, dt_abs = conv_th, conv, conv_th
        w1_stage = [buf[:, i, :, :].rearrange("p h t -> p (h t)")[:, j * H:(j + 1) * H]
                    for buf in (decay, inject) for i in range(2) for j in range(NH * T // H)]
        in_stage = state[:, 0, 0, 0:2 * DI]
        m_norm = conv[:, :, :].rearrange("p h (q d) -> p (h q) d", d=D)

        mask_dram = nc.dram_tensor("mask_dram", (3, E, T), f32).ap()

        def pb(name):
            return ctx.enter_context(nc.psum_tensor(name, [P, T], f32))

        z_ps = [pb("z_ps0"), pb("z_ps1")]
        ye_ps = [pb("ye_ps0"), pb("ye_ps1")]
        fs_ps = pb("fs_ps")
        ms_ps = pb("ms_ps")
        b_ps = pb("b_ps")
        c_ps = pb("c_ps")

        ld_x = [sem(f"ld_x{b}") for b in range(B)]
        ld_w1 = [sem(f"ld_w1_{e}") for e in range(E)]
        ld_w2 = [sem(f"ld_w2_{i}") for i in range(4)]
        ld_small = sem("ld_small")
        ld_mix = sem("ld_mix")
        w1_hi_done = sem("w1_hi_done")
        w1_lo_done = sem("w1_lo_done")
        vec_turned = sem("vec_turned")
        vec_ready = sem("vec_ready")
        const_set = sem("const_set")
        spread_set = sem("spread_set")
        mix_prep = sem("mix_prep")
        mix_exp = sem("mix_exp")
        mix_split = sem("mix_split")
        x_written = sem("x_written")

        f_ln, f_pow = sem("f_ln"), sem("f_pow")
        f_turned, f_copied, f_hi, f_lo = sem("f_turned"), sem("f_copied"), sem("f_hi"), sem("f_lo")
        f_gated, f_route, f_exp = sem("f_gated"), sem("f_route"), sem("f_exp")
        f_bias = sem("f_bias")
        f_mturned, f_mcopied = sem("f_mturned"), sem("f_mcopied")
        mask_out, mask_in = sem("mask_out"), [sem(f"mask_in{c}") for c in range(E // 2)]
        f_up, f_relu, f_down = sem("f_up"), sem("f_relu"), sem("f_down")
        f_scaled, f_added, f_back = sem("f_scaled"), sem("f_added"), sem("f_back")

        m_ln, m_pow = sem("m_ln"), sem("m_pow")
        m_turned, m_hi, m_lo = sem("m_turned"), sem("m_hi"), sem("m_lo")
        m_inproj, m_evac, m_conv, m_tanh = sem("m_inproj"), sem("m_evac"), sem("m_conv"), sem("m_tanh")
        m_gz, m_u, m_xproj, m_bchi, m_bclo = sem("m_gz"), sem("m_u"), sem("m_xproj"), sem("m_bchi"), sem("m_bclo")
        m_dtproj, m_soft, m_dt, m_dtu = sem("m_dtproj"), sem("m_soft"), sem("m_dt"), sem("m_dtu")
        m_B, m_C, m_decay, m_inject = sem("m_B"), sem("m_C"), sem("m_decay"), sem("m_inject")
        m_scan, m_read, m_sum = sem("m_scan"), sem("m_read"), sem("m_sum")
        m_y, m_outproj = sem("m_y"), sem("m_outproj")
        stored = sem("stored")

        def pass_steps(n, own, following, last=False):
            steps = []
            for i in range(UNITS):
                steps.append(("F", i, n))
                if n > 0:
                    steps += [("F", name, n - 1) for name, at in END.items() if at == i]
                steps += [("F", name, n) for name, at in own.items() if at == i]
                steps += [("F", ("scale", e), n) for e in range(E - 1) if i == SCALE_AT(e)]
                steps += [("F", ("add", e), n) for e in range(1, E - 1) if i == SCALE_AT(e) + 1]
                steps += [("F", name, n + 1) for name, at in following.items() if at == i]
            steps.append(("F", "tail", n))
            steps += [("F", name, n) for name in END] if last else [("F", "split", n + 1)]
            return steps

        END = {("scale", E - 1): 1, ("add", E - 1): 2, "epi": 4}

        def SCALE_AT(e):
            return max(HT * e + HT + 2, 2 * HT + 1)

        EARLY_HEAD = dict(ln=7, turn=11, gate=13, route=14, mask=20, bias=21)
        LATE_MASK = dict(gate=0, route=0, mask=5, bias=6)
        FIRST = [("F", s, 0) for s in ("ln", "turn", "split")] + pass_steps(0, LATE_MASK, dict(ln=10, turn=14))
        LOOP_F = (pass_steps(1, LATE_MASK, EARLY_HEAD) + pass_steps(2, {}, dict(ln=28, turn=30))
                  + pass_steps(3, LATE_MASK, dict(ln=27, turn=30)))
        LAST = pass_steps(1, LATE_MASK, {}, last=True)

        M_PLAN = [(None, 5), ("ln", 0, 2.0), ("turn", 0, 1.5)]
        M_PLAN += [(("inproj", j), 0, 1) for j in range(2 * NH)] + [("conv", 0, 4), ("xproj", 0, 0.5),
                                                                    ("dtproj", 0, 1), ("soft", 0, 1)]
        EARLY = {S - 7: ["ln"], S - 6: ["turn"], S - 5: [("inproj", 0)], S - 4: [("inproj", 1)],
                 S - 3: [("inproj", 2)], S - 2: [("inproj", 3)], S - 1: ["conv"]}
        for st in range(S):
            M_PLAN += [(name, 1, 0) for name in EARLY.get(st, [])] + [(st, 0, 2.0 if st else 2.0)]
        M_PLAN += [("xproj", 1, 1), ("gather", 0, 1.5), ("dtproj", 1, 1), ("epi", 0, 1), ("soft", 1, 1)]
        M_PLAN += [(st, 1, 2.0 if st else 2.0) for st in range(S)] + [("gather", 1, 2.5), ("epi", 1, 0)]

        def weave():
            steps, at, units = [], 0, 0
            for name, *place in M_PLAN:
                if name is not None:
                    steps.append(("M", name, place[0]))
                units += place[-1]
                while at < len(LOOP_F) and not (isinstance(LOOP_F[at][1], int)
                                                and UNITS * (LOOP_F[at][2] - 1) + LOOP_F[at][1] >= int(units)):
                    steps.append(LOOP_F[at])
                    at += 1
            return steps + LOOP_F[at:]

        LOOP = weave()

        def behind(later, earlier):
            assert LOOP.index(later) > LOOP.index(earlier), (later, earlier)

        behind(("M", "ln", 0), ("F", "epi", 0))
        behind(("M", "ln", 1), ("F", "epi", 1))
        behind(("F", "ln", 3), ("M", "epi", 0))
        behind(("F", "ln", 4), ("M", "epi", 1))
        LOOP_PASSES = 3
        WRITES = ("bias", "epi")

        def written(steps, upto=None):
            return sum(st[1] in WRITES for st in steps[:upto])

        def run(step_f, step_m, fori):
            for i, (_, st, n) in enumerate(FIRST):
                step_f(st, n, n, n % 3, written(FIRST, i))
            with fori(0, 2) as k:
                for i, (kind, st, n) in enumerate(LOOP):
                    w = None
                    if st in WRITES + ("ln", "mask"):
                        w = k * written(LOOP) + (written(FIRST) + written(LOOP, i))
                    if kind == "F":
                        b = k * -1 + n if 1 <= n <= 3 else k * 3
                        step_f(st, k * LOOP_PASSES + n, b, n % 3, w)
                    else:
                        step_m(st, k * 2 + n, n, w)
            for i, (_, st, n) in enumerate(LAST):
                step_f(st, 2 * B - 2 + n, B - 2 + n, n % 3, written(FIRST) + 2 * written(LOOP) + written(LAST, i))

        def at_start(g):
            return isinstance(g, int) and g == 0

        block = ctx.enter_context(nc.Block())

        @block.sync
        def _(sp):
            xv = x.rearrange("b (t p) d -> b p t d", p=P)
            ov = out.rearrange("b (t p) d -> b p t d", p=P)
            sp.dma_start(xres[:, 0, :, :], xv[0]).then_inc(ld_x[0], 16)
            sp.dma_start(ident[:, :], ident_in).then_inc(ld_small, 16)
            sp.dma_start(w_gate[:, :], W_gate).then_inc(ld_small, 16)
            sp.dma_start(vec_rows[0:UNITS, :], b1.rearrange("e (h p) -> (e h) p", p=P)).then_inc(ld_small, 16)
            for i, v in enumerate((conv_b, dt_proj_b, D_param)):
                sp.dma_start(vec_rows[UNITS + i * NH:UNITS + (i + 1) * NH, :],
                             v.rearrange("(h p) -> h p", p=P)).then_inc(ld_small, 16)
            sp.dma_start(b2_sb[:, :], b2).then_inc(ld_small, 16)
            for e in range(E):
                sp.dma_start(w1_stage[e], W1[e]).then_inc(ld_w1[e], 16)
                if e % 2 == 1:
                    sp.dma_start(w2[:, e - 1:e + 1, :, :],
                                 W2[e - 1:e + 1].rearrange("e (h p) d -> p e h d", p=P)).then_inc(ld_w2[e // 2], 16)
            for b in range(1, B):
                sp.dma_start(xres[:, b, :, :], xv[b]).then_inc(ld_x[b], 16)
            sp.dma_start(in_stage, in_proj_w).then_inc(ld_mix, 16)
            sp.dma_start(conv_sb[:, :, :], conv_w.rearrange("(h p) k -> p h k", p=P)).then_inc(ld_mix, 16)
            xpv = x_proj_w.rearrange("(h p) r -> p h r", p=P)
            sp.dma_start(xproj_sb[:, :, 0:2 * S], xpv[:, :, R:R + 2 * S]).then_inc(ld_mix, 16)
            sp.dma_start(xproj_sb[:, :, 2 * S:], xpv[:, :, 0:R]).then_inc(ld_mix, 16)
            sp.dma_start(dtw_sb[2 * S:, :], dt_proj_w).then_inc(ld_mix, 16)
            sp.dma_start(alog_sb[:, :, :], A_log.rearrange("(h p) s -> p h s", p=P)).then_inc(ld_mix, 16)
            sp.dma_start(outp_sb[:, :, :], out_proj_w.rearrange("(h p) d -> p h d", p=P)).then_inc(ld_mix, 16)

            def step_f(st, g, b, r, w):
                if st != "mask":
                    return
                sp.wait_ge(f_mcopied, g + 1)
                sp.dma_start(mask_dram[r], maskT[:, :]).then_inc(mask_out, 16)
                for c in range(E // 2):
                    if c == 0:
                        sp.wait_ge(mask_out, 16 * g + 16)
                    elif not at_start(g):
                        sp.wait_ge(f_scaled, E * g - (E - 2 * c - 2))
                    sp.dma_start(mask_bc[:, 2 * c:2 * c + 2, :].rearrange("p e t -> p (e t)"),
                                 mask_dram[r, 2 * c:2 * c + 2, :].rearrange("e t -> (e t)").partition_broadcast(P))\
                        .then_inc(mask_in[c], 16)

            run(step_f, lambda *_: None, sp.Fori)
            for b in range(B):
                total = written(FIRST) + 2 * written(LOOP) + written(LAST)
                sp.wait_ge(x_written, total if b == B - 1 else total - 1)
                sp.dma_start(ov[b], xres[:, b, :, :]).then_inc(stored, 16)
            sp.wait_ge(stored, 16 * B)

        @block.gpsimd
        def _(pool):
            nc.gpsimd.memset(neg_half[:, :], -0.5).then_inc(const_set, 1)
            nc.gpsimd.memset(xpad[:, :, 0:TAPS - 1], 0.0).then_inc(const_set, 1)
            pool.wait_ge(const_set, 2)

            def make_spread():
                pool.wait_ge(ld_small, 112)
                for r in (0, 2 * S):
                    if r:
                        pool.wait_ge(spread_set, 1)
                    src = ident[r:r + 2 * S, r:r + 2 * S].unsqueeze(2).to_broadcast([2 * S, 2 * S, P])
                    nc.gpsimd.tensor_copy(spread[r:r + 2 * S, :, :], src).then_inc(spread_set, 1)
                pool.wait_ge(spread_set, 2)

            def step_f(st, g, b, r, w):
                if st == "ln":
                    pool.wait_ge(f_ln, 4 * g + 3)
                    nc.gpsimd.tensor_tensor(f_rstd[:, :], f_var[:, :], neg_half[:, :], ALU.pow).then_inc(f_pow, 1)
                if at_start(g) and st == HT:
                    make_spread()
                if isinstance(st, tuple) and st[0] == "add":
                    add(g, st[1])

            def add(g, e):
                pool.wait_ge(f_scaled, E * g + e + 1)
                if e >= 2:
                    pool.wait_ge(f_added, (E - 1) * g + e - 1)
                nc.gpsimd.tensor_tensor(y_sum[:, :], y_sum[:, :], y_part[:, e % 2, :], ALU.add).then_inc(f_added, 1)

            def step_m(st, m, h2, w):
                if st == "ln":
                    pool.wait_ge(m_ln, 4 * m + 3)
                    nc.gpsimd.tensor_tensor(m_rstd[:, :], m_var[:, :], neg_half[:, :], ALU.pow).then_inc(m_pow, 1)
                if isinstance(st, int) and st >= 1:
                    pool.wait_ge(m_read, S * m + st + 1)
                    if st >= 2:
                        pool.wait_ge(m_sum, (S - 1) * m + st - 1)
                    nc.gpsimd.tensor_tensor(y_ssm[:, :, :], y_ssm[:, :, :], read[:, st % 2, :, :], ALU.add)\
                        .then_inc(m_sum, 1)

            run(step_f, step_m, pool.Fori)

        @block.scalar
        def _(act):
            act.wait_ge(vec_turned, 1)
            nc.scalar.copy(vec_cols[:, :], fs_ps[:, 0:VECS]).then_inc(vec_ready, 1)

            def w1_high(e):
                act.wait_ge(ld_w1[e], 16)
                nc.scalar.copy(w1_hi[:, e, :], w1_stage[e]).then_inc(w1_hi_done, 1)

            def mixer_weights():
                act.wait_ge(ld_mix, 112)
                nc.scalar.copy(in_hi[:, :], in_stage).then_inc(mix_exp, 1)
                nc.scalar.activation(aexp_sb[:, :, :], alog_sb[:, :, :], ACT.Exp).then_inc(mix_exp, 1)

            def step_f(st, g, b, r, w):
                if st == "turn":
                    act.wait_ge(f_turned, g + 1)
                    nc.scalar.copy(f_xT[:, :], fs_ps[:, :]).then_inc(f_copied, 1)
                if st == "split":
                    act.wait_ge(f_copied, g + 1)
                    nc.scalar.copy(f_xhi[:, :], f_xT[:, :]).then_inc(f_hi, 1)
                    if at_start(g):
                        w1_high(0)
                        w1_high(1)
                if st == "route":
                    act.wait_ge(f_route, 8 * g + 3)
                    nc.scalar.activation(gexp[:, :, :], gshift[:, :, :], ACT.Exp).then_inc(f_exp, 1)
                if st == "mask":
                    act.wait_ge(f_mturned, g + 1)
                    nc.scalar.copy(maskT[:, :], fs_ps[0:E, :]).then_inc(f_mcopied, 1)
                if isinstance(st, int):
                    if at_start(g) and st % HT == 0 and st // HT + 2 < E:
                        w1_high(st // HT + 2)
                    if at_start(g) and st == 5 * HT + 2:
                        mixer_weights()
                    act.wait_ge(f_up, UNITS * g + st + 1)
                    if not (at_start(g) and st < NHB):
                        act.wait_ge(f_down, UNITS * g + st - NHB + 1)
                    nc.scalar.activation(hid[:, st % NHB, :], z_ps[st % 2][:, :], ACT.Relu,
                                         bias=vec_cols[:, st:st + 1]).then_inc(f_relu, 1)

            def decays(m, s):
                if s == 0:
                    act.wait_ge(m_dt, m + 1)
                if not (isinstance(m, int) and m == 0 and s < 2):
                    if s >= 2:
                        act.wait_ge(m_scan, NH * (S * m + s - 1))
                for h in range(NH):
                    nc.scalar.activation(decay[:, s % 2, h, :], dt[:, h, :], ACT.Exp,
                                         scale=a_neg[:, h, s:s + 1]).then_inc(m_decay, 1)

            def step_m(st, m, h2, w):
                if st == "turn":
                    act.wait_ge(m_turned, m + 1)
                    nc.scalar.copy(m_xhi[:, :], ms_ps[:, :]).then_inc(m_hi, 1)
                if isinstance(st, tuple) and st[0] == "inproj":
                    j = st[1]
                    act.wait_ge(m_inproj, 2 * NH * m + j + 1)
                    if j < NH:
                        nc.scalar.copy(xpad[:, j, TAPS - 1:], ms_ps[:, :]).then_inc(m_evac, 1)
                    else:
                        nc.scalar.copy(zg[:, h2, j - NH, :], ms_ps[:, :])
                        nc.scalar.activation(z_th[:, j - NH, :], ms_ps[:, :], ACT.Tanh, scale=0.5).then_inc(m_evac, 1)
                if st == "conv":
                    act.wait_ge(m_conv, NH * TAPS * m + NH * TAPS)
                    act.wait_ge(m_gz, m + 1)
                    nc.scalar.activation(conv_th[:, :, :], conv[:, :, :], ACT.Tanh).then_inc(m_tanh, 1)
                if st == "xproj":
                    act.wait_ge(m_xproj, m + 1)
                    nc.scalar.copy(bc[0:2 * S, :], ms_ps[0:2 * S, :]).then_inc(m_bchi, 1)
                    nc.scalar.copy(dt_low[2 * S:, :], ms_ps[2 * S:2 * S + R, :]).then_inc(m_bchi, 1)
                if st == "dtproj":
                    for h in range(NH):
                        ps = (b_ps, c_ps)[h]
                        act.wait_ge(m_dtproj, NH * m + h + 1)
                        nc.scalar.activation(dt_lin[:, h, :], ps[:, :], ACT.Identity, bias=dtb_sb[:, h:h + 1])
                        nc.scalar.activation(dt_abs[:, h, :], ps[:, :], ACT.Abs, bias=dtb_sb[:, h:h + 1])\
                            .then_inc(m_soft, 1)
                    act.wait_ge(m_soft, 4 * m + 2)
                    nc.scalar.activation(dt_abs[:, :, :], dt_abs[:, :, :], ACT.Exp, scale=-1.0).then_inc(m_soft, 1)
                    act.wait_ge(m_soft, 4 * m + 3)
                    nc.scalar.activation(dt_abs[:, :, :], dt_abs[:, :, :], ACT.Ln, bias=1.0).then_inc(m_soft, 1)
                if st == "soft":
                    decays(m, 0)
                if isinstance(st, int) and st + 1 < S:
                    decays(m, st + 1)

            run(step_f, step_m, act.Fori)

        @block.tensor
        def _(pe):
            pe.wait_ge(ld_small, 112)
            nc.tensor.transpose(fs_ps[:, 0:VECS], vec_rows[:, :], ident[0:VECS, 0:VECS]).then_inc(vec_turned, 1)
            pe.wait_ge(vec_ready, 1)

            def down(g, i):
                e, ht = i // HT, i % HT
                pe.wait_ge(f_relu, UNITS * g + i + 1)
                if ht == 0 and not (at_start(g) and e < 2):
                    pe.wait_ge(f_scaled, E * g + e - 1)
                if at_start(g) and ht == 0 and e % 2 == 0:
                    pe.wait_ge(ld_w2[e // 2], 16)
                nc.tensor.matmul(ye_ps[e % 2][:, :], w2[:, e, ht, :], hid[:, i % NHB, :],
                                 start=(ht == 0), stop=(ht == HT - 1)).then_inc(f_down, 1)

            def step_f(st, g, b, r, w):
                if st == "turn":
                    pe.wait_ge(f_ln, 4 * g + 4)
                    for t in range(TT):
                        mm = nc.tensor.transpose(fs_ps[:, t * P:(t + 1) * P], f_norm[:, t, :], ident[:, :])
                    mm.then_inc(f_turned, 1)
                if st == "gate":
                    pe.wait_ge(f_copied, g + 1)
                    for t in range(TT):
                        mm = nc.tensor.matmul(fs_ps[:, t * E:(t + 1) * E], f_xT[:, t * P:(t + 1) * P], w_gate[:, :],
                                              start=True, stop=True)
                    mm.then_inc(f_gated, 1)
                if st == "mask":
                    pe.wait_ge(f_route, 8 * g + 8)
                    if not at_start(g):
                        pe.wait_ge(x_written, w)
                    for t in range(TT):
                        mm = nc.tensor.transpose(fs_ps[0:E, t * P:(t + 1) * P], mask[:, t, :], ident[:, :])
                    mm.then_inc(f_mturned, 1)
                if isinstance(st, int):
                    e = st // HT
                    if st == 0:
                        pe.wait_ge(f_lo, g + 1)
                    if at_start(g) and st % HT == 0:
                        pe.wait_ge(w1_lo_done, e + 1)
                    if not (at_start(g) and st < 2):
                        pe.wait_ge(f_relu, UNITS * g + st - 1)
                    cols = slice((st % HT) * P, (st % HT + 1) * P)
                    for i, (w, v) in enumerate(((w1_hi, f_xhi), (w1_hi, f_xlo), (w1_lo, f_xhi))):
                        mm = nc.tensor.matmul(z_ps[st % 2][:, :], w[:, e, cols], v[:, :], start=(i == 0), stop=(i == 2))
                    mm.then_inc(f_up, 1)
                    if st >= 2:
                        down(g, st - 2)
                if st == "tail":
                    down(g, UNITS - 2)
                    down(g, UNITS - 1)
                if st == "epi":
                    pe.wait_ge(f_added, (E - 1) * g + E - 1)
                    for t in range(TT):
                        cols = slice(t * P, (t + 1) * P)
                        mm = nc.tensor.transpose(fs_ps[:, cols], y_sum[:, cols], ident[:, :])
                    mm.then_inc(f_back, 1)
                if st == "bias":
                    pe.wait_ge(f_mcopied, g + 1)
                    for t in range(TT):
                        cols = slice(t * P, (t + 1) * P)
                        mm = nc.tensor.matmul(fs_ps[:, cols], maskT[:, cols], b2_sb[:, :], start=True, stop=True)
                    mm.then_inc(f_bias, 1)

            def spread_row(ps, j):
                return nc.tensor.matmul(ps[:, :], spread[:, j, :], bc[:, :], start=True, stop=True)

            def step_m(st, m, h2, w):
                if st == "turn":
                    pe.wait_ge(m_ln, 4 * m + 4)
                    for t in range(TT):
                        mm = nc.tensor.transpose(ms_ps[:, t * P:(t + 1) * P], m_norm[:, t, :], ident[:, :])
                    mm.then_inc(m_turned, 1)
                if isinstance(st, tuple) and st[0] == "inproj":
                    j = st[1]
                    if j == 0:
                        pe.wait_ge(m_lo, m + 1)
                        pe.wait_ge(mix_split, 1)
                    else:
                        pe.wait_ge(m_evac, 2 * NH * m + j)
                    cols = slice(j * P, (j + 1) * P)
                    for i, (w_, v) in enumerate(((in_hi, m_xhi), (in_hi, m_xlo), (in_lo, m_xhi))):
                        mm = nc.tensor.matmul(ms_ps[:, :], w_[:, cols], v[:, :], start=(i == 0), stop=(i == 2))
                    mm.then_inc(m_inproj, 1)
                if st == "xproj":
                    pe.wait_ge(m_u, m + 1)
                    pe.wait_ge(m_evac, 2 * NH * m + 4)
                    for h in range(NH):
                        mm = nc.tensor.matmul(ms_ps[0:2 * S + R, :], xproj_sb[:, h, :], u[:, h2, h, :],
                                              start=(h == 0), stop=(h == NH - 1))
                    mm.then_inc(m_xproj, 1)
                if st == "dtproj":
                    pe.wait_ge(m_bchi, 2 * m + 2)
                    if h2 == 1:
                        pe.wait_ge(m_read, S * m)
                    for h in range(NH):
                        ps = (b_ps, c_ps)[h]
                        nc.tensor.matmul(ps[:, :], dtw_sb[2 * S:, h * P:(h + 1) * P], dt_low[2 * S:, :],
                                         start=True, stop=True).then_inc(m_dtproj, 1)
                if st == "soft":
                    pe.wait_ge(m_bclo, m + 1)
                    pe.wait_ge(m_soft, 4 * m + 2)
                    pe.wait_ge(spread_set, 2)
                    spread_row(b_ps, 0).then_inc(m_B, 1)
                if isinstance(st, int):
                    if st >= 1:
                        pe.wait_ge(m_read, S * m + st)
                    spread_row(c_ps, S + st).then_inc(m_C, 1)
                    if st + 1 < S:
                        pe.wait_ge(m_inject, S * m + st + 1)
                        spread_row(b_ps, st + 1).then_inc(m_B, 1)
                if st == "epi":
                    pe.wait_ge(m_y, 3 * m + 3)
                    for t in range(TT):
                        cols = slice(t * P, (t + 1) * P)
                        for h in range(NH):
                            mm = nc.tensor.matmul(ms_ps[:, cols], y_ssm[:, h, cols], outp_half[:, h, :],
                                                  start=(h == 0), stop=(h == NH - 1))
                    mm.then_inc(m_outproj, 1)

            run(step_f, step_m, pe.Fori)

        @block.vector
        def _(dve):
            def w1_low(e):
                dve.wait_ge(w1_hi_done, e + 1)
                nc.vector.tensor_tensor(w1_lo[:, e, :], w1_stage[e], w1_hi[:, e, :].bitcast(f32), ALU.subtract)\
                    .then_inc(w1_lo_done, 1)

            def mixer_weights():
                dve.wait_ge(mix_exp, 2)
                nc.vector.tensor_tensor(in_lo[:, :], in_stage, in_hi[:, :].bitcast(f32), ALU.subtract).then_inc(mix_split, 1)
                nc.vector.tensor_scalar(a_neg[:, :, :], aexp_sb[:, :, :], -1.0, None, ALU.mult).then_inc(mix_prep, 1)
                nc.vector.tensor_scalar(conv_half[:, :, :], conv_sb[:, :, :], 0.5, None, ALU.mult).then_inc(mix_prep, 1)
                nc.vector.tensor_scalar(convb_half[:, :], convb_sb[:, :], 0.5, None, ALU.mult).then_inc(mix_prep, 1)
                nc.vector.tensor_scalar(outp_half[:, :, :], outp_sb[:, :, :], 0.5, None, ALU.mult).then_inc(mix_prep, 1)
                dve.wait_ge(mix_prep, 4)

            def layer_norm(src, stat, mv, var, rstd, norm, ln, power, n):
                nc.vector.memset(unused[:, :], 0.0)
                for t in range(TT):
                    ins = nc.vector.bn_stats(stat[:, t, :], src(t))
                ins.then_inc(ln, 1)
                dve.wait_ge(ln, 4 * n + 1)
                nc.vector.memset(unused[:, :], 0.0)
                for t in range(TT):
                    ins = nc.vector.bn_aggr(mv[:, t, :], stat[:, t, :])
                ins.then_inc(ln, 1)
                dve.wait_ge(ln, 4 * n + 2)
                nc.vector.tensor_scalar(var[:, :], mv[:, :, 1], EPS, None, ALU.add).then_inc(ln, 1)
                dve.wait_ge(power, n + 1)
                for t in range(TT):
                    ins = nc.vector.tensor_scalar(norm[:, t, :], src(t), mv[:, t, 0:1], rstd[:, t:t + 1],
                                                  ALU.subtract, ALU.mult)
                ins.then_inc(ln, 1)

            def per_token(v, j):
                return v[:, :, j:j + 1].to_broadcast([P, TT, E])

            def scale(g, e):
                dve.wait_ge(f_down, UNITS * g + HT * (e + 1))
                if e % 2 == 0:
                    dve.wait_ge(mask_in[e // 2], 16 * g + 16)
                if e >= 3:
                    dve.wait_ge(f_added, (E - 1) * g + e - 2)
                dst = y_sum[:, :] if e == 0 else y_part[:, e % 2, :]
                nc.vector.tensor_tensor(dst, ye_ps[e % 2][:, :], mask_bc[:, e, :], ALU.mult).then_inc(f_scaled, 1)

            def step_f(st, g, b, r, w):
                if st == "ln":
                    if isinstance(g, int) and g < B:
                        dve.wait_ge(ld_x[g], 16)
                        if g == 1:
                            for later in ld_x[2:]:
                                dve.wait_ge(later, 16)
                    if not at_start(g):
                        dve.wait_ge(x_written, w)
                    layer_norm(lambda t: xres[:, b, t, :], f_stat, f_mv, f_var, f_rstd, f_norm, f_ln, f_pow, g)
                if st == "split":
                    dve.wait_ge(f_hi, g + 1)
                    nc.vector.tensor_tensor(f_xlo[:, :], f_xT[:, :], f_xhi[:, :].bitcast(f32), ALU.subtract)\
                        .then_inc(f_lo, 1)
                    if at_start(g):
                        w1_low(0)
                        w1_low(1)
                if st == "route":
                    q = 8 * g
                    dve.wait_ge(f_gated, g + 1)
                    nc.vector.tensor_copy(gate[:, :, :], fs_ps[:, 0:TT * E].rearrange("p (t e) -> p t e", e=E))\
                        .then_inc(f_route, 1)
                    dve.wait_ge(f_route, q + 1)
                    nc.vector.memset(unused[:, :], 0.0)
                    for t in range(TT):
                        ins = nc.vector.max(top[:, t, :], gate[:, t, :])
                    ins.then_inc(f_route, 1)
                    dve.wait_ge(f_route, q + 2)
                    nc.vector.tensor_tensor(gshift[:, :, :], gate[:, :, :], per_token(top, 0), ALU.subtract).then_inc(f_route, 1)
                    nc.vector.tensor_tensor(gkeep[:, :, :], gate[:, :, :], per_token(top, 1), ALU.is_ge).then_inc(f_route, 1)
                    dve.wait_ge(f_route, q + 4)
                    dve.wait_ge(f_exp, g + 1)
                    nc.vector.tensor_tensor(gexp[:, :, :], gexp[:, :, :], gkeep[:, :, :], ALU.mult).then_inc(f_route, 1)
                    dve.wait_ge(f_route, q + 5)
                    nc.vector.tensor_reduce(gsum[:, :], gexp[:, :, :], AX.X, ALU.add).then_inc(f_route, 1)
                    dve.wait_ge(f_route, q + 6)
                    nc.vector.reciprocal(grec[:, :], gsum[:, :]).then_inc(f_route, 1)
                    dve.wait_ge(f_route, q + 7)
                    nc.vector.scalar_tensor_tensor(out=mask[:, :, :], in0=gexp[:, :, :], scalar=FFN_SCALE,
                                                   in1=grec[:, :].unsqueeze(2).to_broadcast([P, TT, E]),
                                                   op0=ALU.mult, op1=ALU.mult).then_inc(f_route, 1)
                if at_start(g) and isinstance(st, int) and st % HT == 0 and st // HT + 2 < E:
                    w1_low(st // HT + 2)
                if at_start(g) and st == 5 * HT + 2:
                    mixer_weights()
                if isinstance(st, tuple) and st[0] == "scale":
                    scale(g, st[1])
                if st == "bias":
                    dve.wait_ge(f_bias, g + 1)
                    if not at_start(g):
                        dve.wait_ge(x_written, w)
                    xb = xres[:, b, :, :].rearrange("p t d -> p (t d)")
                    nc.vector.tensor_tensor(xb, fs_ps[:, :], xb, ALU.add).then_inc(x_written, 1)
                if st == "epi":
                    dve.wait_ge(f_back, g + 1)
                    dve.wait_ge(x_written, w)
                    xb = xres[:, b, :, :].rearrange("p t d -> p (t d)")
                    nc.vector.tensor_tensor(xb, fs_ps[:, :], xb, ALU.add).then_inc(x_written, 1)

            def halves(ps):
                return ps[:, :].unsqueeze(1).to_broadcast([P, NH, T])

            def inject_step(m, s):
                dve.wait_ge(m_B, S * m + s + 1)
                nc.vector.tensor_tensor(inject[:, s % 2, :, :], dtu[:, :, :], halves(b_ps), ALU.mult).then_inc(m_inject, 1)

            def step_m(st, m, h2, w):
                if st == "ln":
                    dve.wait_ge(x_written, w)
                    layer_norm(lambda t: xres[:, m, t, :], m_stat, m_mv, m_var, m_rstd, m_norm, m_ln, m_pow, m)
                if st == "turn":
                    dve.wait_ge(m_hi, m + 1)
                    nc.vector.tensor_tensor(m_xlo[:, :], ms_ps[:, :], m_xhi[:, :].bitcast(f32), ALU.subtract)\
                        .then_inc(m_lo, 1)
                if st == "conv":
                    dve.wait_ge(m_evac, 2 * NH * m + NH)
                    dve.wait_ge(const_set, 2)
                    for k in range(TAPS):
                        for h in range(NH):
                            n = NH * k + h
                            if k == 0:
                                ins = nc.vector.tensor_scalar(conv[:, h, :], xpad[:, h, 0:T], conv_half[:, h, 0:1],
                                                              convb_half[:, h:h + 1], ALU.mult, ALU.add)
                            else:
                                dve.wait_ge(m_conv, NH * TAPS * m + n - 1)
                                ins = nc.vector.scalar_tensor_tensor(
                                    out=conv[:, h, :], in0=xpad[:, h, k:k + T], scalar=conv_half[:, h, k:k + 1],
                                    in1=conv[:, h, :], op0=ALU.mult, op1=ALU.add)
                            ins.then_inc(m_conv, 1)
                    dve.wait_ge(m_evac, 2 * NH * m + 2 * NH)
                    nc.vector.scalar_tensor_tensor(out=zg[:, h2], in0=z_th[:, :, :], scalar=1.0, in1=zg[:, h2],
                                                   op0=ALU.add, op1=ALU.mult).then_inc(m_gz, 1)
                    dve.wait_ge(m_tanh, m + 1)
                    nc.vector.scalar_tensor_tensor(out=u[:, h2], in0=conv_th[:, :, :], scalar=1.0, in1=conv[:, :, :],
                                                   op0=ALU.add, op1=ALU.mult).then_inc(m_u, 1)
                if st == "xproj":
                    dve.wait_ge(m_bchi, 2 * m + 1)
                    nc.vector.tensor_tensor(bc[2 * S:4 * S, :], ms_ps[0:2 * S, :], bc[0:2 * S, :].bitcast(f32), ALU.subtract)\
                        .then_inc(m_bclo, 1)
                if st == "soft":
                    dve.wait_ge(m_soft, 4 * m + 4)
                    nc.vector.scalar_tensor_tensor(out=dt[:, :, :], in0=dt_lin[:, :, :], scalar=0.0, in1=dt_abs[:, :, :],
                                                   op0=ALU.max, op1=ALU.add).then_inc(m_dt, 1)
                    dve.wait_ge(m_dt, m + 1)
                    dve.wait_ge(m_u, m + 1)
                    nc.vector.tensor_tensor(dtu[:, :, :], dt[:, :, :], u[:, h2], ALU.mult).then_inc(m_dtu, 1)
                    dve.wait_ge(m_dtu, m + 1)
                    inject_step(m, 0)
                if isinstance(st, int):
                    n = S * m + st
                    dve.wait_ge(m_inject, n + 1)
                    for h in range(NH):
                        dve.wait_ge(m_decay, NH * n + h + 1)
                        nc.vector.tensor_tensor_scan(state[:, st % 2, h, :], decay[:, st % 2, h, :],
                                                     inject[:, st % 2, h, :], 0.0, ALU.mult, ALU.add).then_inc(m_scan, 1)
                    if st + 1 < S:
                        inject_step(m, st + 1)
                    dve.wait_ge(m_scan, NH * n + NH)
                    dve.wait_ge(m_C, n + 1)
                    if st >= 3:
                        dve.wait_ge(m_sum, (S - 1) * m + st - 2)
                    dst = y_ssm[:, :, :] if st == 0 else read[:, st % 2, :, :]
                    nc.vector.tensor_tensor(dst, state[:, st % 2, :, :], halves(c_ps), ALU.mult).then_inc(m_read, 1)
                if st == "gather":
                    dve.wait_ge(m_sum, (S - 1) * m + S - 1)
                    for h in range(NH):
                        ins = nc.vector.scalar_tensor_tensor(out=y_ssm[:, h, :], in0=u[:, h2, h, :], scalar=dskip_sb[:, h:h + 1],
                                                             in1=y_ssm[:, h, :], op0=ALU.mult, op1=ALU.add)
                        ins.then_inc(m_y, 1)
                    dve.wait_ge(m_y, 3 * m + 2)
                    dve.wait_ge(m_gz, m + 1)
                    nc.vector.tensor_tensor(y_ssm[:, :, :], y_ssm[:, :, :], zg[:, h2], ALU.mult).then_inc(m_y, 1)
                if st == "epi":
                    dve.wait_ge(m_outproj, m + 1)
                    dve.wait_ge(x_written, w)
                    xb = xres[:, m, :, :].rearrange("p t d -> p (t d)")
                    nc.vector.tensor_tensor(xb, ms_ps[:, :], xb, ALU.add).then_inc(x_written, 1)

            run(step_f, step_m, dve.Fori)


_INS = ["L0_attn_x", "L0_attn_in_proj_w", "L0_attn_conv_w", "L0_attn_conv_b", "L0_attn_x_proj_w",
        "L0_attn_dt_proj_w", "L0_attn_dt_proj_b", "L0_attn_A_log", "L0_attn_D_param", "L0_attn_out_proj_w",
        "L0_ffn_W_gate", "L0_ffn_W1", "L0_ffn_b1", "L0_ffn_W2", "L0_ffn_b2"]


def kernel(**inputs):
    import numpy as _np
    import concourse.bacc as _bacc
    from concourse import mybir as _mybir
    from concourse.bass_utils import run_bass_kernel_spmd as _run

    nc = _bacc.Bacc("TRN2", target_bir_lowering=False, num_devices=1)
    arrays, args = {}, []
    for name in _INS:
        a = _np.ascontiguousarray(inputs[name])
        arrays[f"in_{name}_dram"] = a
        args.append(nc.dram_tensor(f"in_{name}_dram", a.shape, _mybir.dt.from_np(a.dtype), kind="ExternalInput").ap())
    ident = _np.eye(128, dtype=_np.float32)
    arrays["in_ident_dram"] = ident
    args.append(nc.dram_tensor("in_ident_dram", ident.shape, _mybir.dt.float32, kind="ExternalInput").ap())
    shape = tuple(inputs["L0_attn_x"].shape)
    args.append(nc.dram_tensor("out_0_dram", shape, _mybir.dt.float32, kind="ExternalOutput").ap())
    macaron_kernel(nc, *args)
    r = _run(nc, [arrays], core_ids=[0])
    return r.results[0]["out_0_dram"]
```

```python
from contextlib import ExitStack

import concourse.bass as bass
from concourse import mybir


def macaron_kernel(nc, x, in_proj_w, conv_w, conv_b, x_proj_w, dt_proj_w, dt_proj_b, A_log, D_param,
                   out_proj_w, W_gate, W1, b1, W2, b2, ident_in, out):
    f32, f32r = mybir.dt.float32, mybir.dt.float32r
    ALU, ACT, AX = mybir.AluOpType, mybir.ActivationFunctionType, mybir.AxisListType

    P = 128
    B, T, D = x.shape
    TT = T // P
    E, _, H = W1.shape
    HT = H // P
    UNITS = E * HT
    DI = conv_w.shape[0]
    NH = DI // P
    TAPS = conv_w.shape[1]
    S = A_log.shape[1]
    R = dt_proj_w.shape[0]
    EPS = 1e-5
    FFN_SCALE = 0.5 / E

    ctx = ExitStack()
    with ctx:
        def sb(name, shape, dt=f32):
            return ctx.enter_context(nc.sbuf_tensor(name, shape, dt))

        def sem(name):
            return ctx.enter_context(nc.semaphore(name))

        ident = sb("ident", [P, P])
        w1_hi = sb("w1_hi", [P, E, H], f32r)
        w1_lo = sb("w1_lo", [P, E, H], f32r)
        w2 = sb("w2", [P, E, HT, D])
        VECS = UNITS + 3 * NH + E
        vec_rows = sb("vec_rows", [VECS, P])
        vec_cols = sb("vec_cols", [P, VECS])
        w_gate = sb("w_gate", [P, E])
        in_hi = sb("in_hi", [P, 2 * DI], f32r)
        in_lo = sb("in_lo", [P, 2 * DI], f32r)
        conv_sb = sb("conv_sb", [P, NH, TAPS])
        conv_half = sb("conv_half", [P, NH, TAPS])
        convb_half = sb("convb_half", [P, NH])
        xproj_sb = sb("xproj_sb", [P, NH, 2 * S + R])
        dtw_sb = sb("dtw_sb", [2 * S + R, DI])
        alog_sb = sb("alog_sb", [P, NH, S])
        aexp_sb = sb("aexp_sb", [P, NH, S])
        a_neg = sb("a_neg", [P, NH, S])
        convb_sb, dtb_sb, dskip_sb = (vec_cols[:, UNITS + i * NH:UNITS + (i + 1) * NH] for i in range(3))
        b2_cols = vec_cols[:, UNITS + 3 * NH:]
        outp_sb = sb("outp_sb", [P, NH, D])
        outp_half = sb("outp_half", [P, NH, D])
        spread = sb("spread", [4 * S, 2 * S, P], f32r)
        neg_half = sb("neg_half", [P, TT])
        unused = sb("unused", [P, 1])

        xres = sb("xres", [P, B, TT, D])

        f_stat = sb("f_stat", [P, TT, 6])
        f_mv = sb("f_mv", [P, TT, 2])
        f_var = sb("f_var", [P, TT])
        f_rstd = sb("f_rstd", [P, TT])
        f_norm = sb("f_norm", [P, TT, D])
        f_xT = sb("f_xT", [P, T])
        f_xhi = sb("f_xhi", [P, T], f32r)
        f_xlo = sb("f_xlo", [P, T], f32r)
        gate = sb("gate", [P, TT, E])
        top = sb("top", [P, TT, 8])
        gshift = sb("gshift", [P, TT, E])
        gkeep = sb("gkeep", [P, TT, E])
        gexp = sb("gexp", [P, TT, E])
        gsum = sb("gsum", [P, TT])
        grec = sb("grec", [P, TT])
        mask = sb("mask", [P, TT, E])
        maskT = sb("maskT", [E, T])
        mask_bc = sb("mask_bc", [P, E, T])
        NHB = 4
        hid = sb("hid", [P, NHB, T])
        y_part = sb("y_part", [P, 2, T])
        y_sum = sb("y_sum", [P, T])

        m_stat = sb("m_stat", [P, TT, 6])
        m_mv = sb("m_mv", [P, TT, 2])
        m_var = sb("m_var", [P, TT])
        m_rstd = sb("m_rstd", [P, TT])
        m_xhi = sb("m_xhi", [P, T], f32r)
        m_xlo = sb("m_xlo", [P, T], f32r)
        xpad = sb("xpad", [P, NH, TAPS - 1 + T])
        zg = sb("zg", [P, 2, NH, T])
        u = sb("u", [P, NH, T])
        conv = sb("conv", [P, NH, T])
        conv_th = sb("conv_th", [P, NH, T])
        z_th = sb("z_th", [P, NH, T])
        bc = sb("bc", [4 * S, 2, T], f32r)
        dt_low = sb("dt_low", [2 * S + R, T])
        dt = sb("dt", [P, NH, T])
        dtu = sb("dtu", [P, NH, T])
        decay = sb("decay", [P, 2, NH, T])
        inject = sb("inject", [P, 2, NH, T])
        state = sb("state", [P, 2, NH, T])
        read = sb("read", [P, 2, NH, T])
        y_ssm = sb("y_ssm", [P, NH, T])
        dt_lin, dt_abs = conv, conv_th
        w1_stage = [buf[:, i, :, :].rearrange("p h t -> p (h t)")[:, j * H:(j + 1) * H]
                    for buf in (decay, inject) for i in range(2) for j in range(NH * T // H)]
        in_stage = state[:, 0, 0, 0:2 * DI]
        m_norm = conv[:, :, :].rearrange("p h (q d) -> p (h q) d", d=D)

        mask_dram = nc.dram_tensor("mask_dram", (3, E, T), f32).ap()

        def pb(name):
            return ctx.enter_context(nc.psum_tensor(name, [P, T], f32))

        z_ps = [pb("z_ps0"), pb("z_ps1")]
        ye_ps = [pb("ye_ps0"), pb("ye_ps1")]
        fs_ps = pb("fs_ps")
        ms_ps = pb("ms_ps")
        b_ps = pb("b_ps")
        c_ps = pb("c_ps")

        ld_x = [sem(f"ld_x{b}") for b in range(B)]
        ld_w1 = [sem(f"ld_w1_{e}") for e in range(E)]
        ld_w2 = [sem(f"ld_w2_{i}") for i in range(4)]
        ld_ident, ld_small = sem("ld_ident"), sem("ld_small")
        ld_mix = sem("ld_mix")
        w1_hi_done = sem("w1_hi_done")
        w1_lo_done = sem("w1_lo_done")
        vec_turned = sem("vec_turned")
        vec_ready = sem("vec_ready")
        const_set = sem("const_set")
        spread_set = sem("spread_set")
        mix_prep = sem("mix_prep")
        mix_exp = sem("mix_exp")
        mix_split = sem("mix_split")
        x_written = sem("x_written")

        f_ln, f_pow, f_normed = sem("f_ln"), sem("f_pow"), sem("f_normed")
        f_turned, f_copied, f_hi, f_lo = sem("f_turned"), sem("f_copied"), sem("f_hi"), sem("f_lo")
        f_gated, f_route, f_exp = sem("f_gated"), sem("f_route"), sem("f_exp")
        f_mturned, f_mcopied = sem("f_mturned"), sem("f_mcopied")
        mask_out, mask_in = sem("mask_out"), [sem(f"mask_in{c}") for c in range(E // 2)]
        f_up, f_relu, f_down = sem("f_up"), sem("f_relu"), sem("f_down")
        f_scaled, f_added, f_back = sem("f_scaled"), sem("f_added"), sem("f_back")

        m_ln, m_pow, m_normed = sem("m_ln"), sem("m_pow"), sem("m_normed")
        m_turned, m_hi, m_lo = sem("m_turned"), sem("m_hi"), sem("m_lo")
        m_inproj, m_evac, m_tanh = sem("m_inproj"), sem("m_evac"), sem("m_tanh")
        m_tap0, m_conv = sem("m_tap0"), sem("m_conv")
        m_th1 = sem("m_th1")
        m_gz, m_u, m_xproj, m_bchi, m_bclo = sem("m_gz"), sem("m_u"), sem("m_xproj"), sem("m_bchi"), sem("m_bclo")
        m_dtproj, m_soft, m_dt, m_dtu = sem("m_dtproj"), sem("m_soft"), sem("m_dt"), sem("m_dtu")
        m_B, m_C, m_decay, m_inject = sem("m_B"), sem("m_C"), sem("m_decay"), sem("m_inject")
        m_scan, m_read, m_sum = sem("m_scan"), sem("m_read"), sem("m_sum")
        m_skip, m_y, m_outproj = sem("m_skip"), sem("m_y"), sem("m_outproj")
        stored = sem("stored")

        def pass_steps(n, own, following, last=False):
            steps = []
            for i in range(UNITS):
                steps.append(("F", i, n))
                if n > 0:
                    steps += [("F", name, n - 1) for name, at in END.items() if at == i]
                steps += [("F", name, n) for name, at in own.items() if at == i]
                steps += [("F", ("scale", e), n) for e in range(E - 1) if i == SCALE_AT(e)]
                steps += [("F", ("add", e), n) for e in range(1, E - 1) if i == SCALE_AT(e) + 1]
                steps += [("F", name, n + 1) for name, at in following.items() if at == i]
            steps.append(("F", "tail", n))
            steps += [("F", name, n) for name in END] if last else [("F", "split", n + 1)]
            return steps

        END = {("scale", E - 1): 1, ("add", E - 1): 1, "epi": 3}

        def SCALE_AT(e):
            return max(HT * e + HT + 2, 2 * HT + 1)

        FIRST = [("F", s, 0) for s in ("ln", "norm", "turn", "split")]
        FIRST += pass_steps(0, dict(gate=0, route=2, weigh=2, mask=3), dict(ln=14, norm=14, turn=21))
        LOOP_F = pass_steps(1, dict(gate=0, route=2, weigh=4, mask=6),
                            dict(ln=8, norm=8, turn=10, gate=11, route=12, weigh=18, mask=19))
        LOOP_F += pass_steps(2, {}, dict(ln=29, norm=29, turn=31))
        LOOP_F += pass_steps(3, dict(gate=0, route=1, weigh=2, mask=4), dict(ln=28, norm=30, turn=31))
        LAST = pass_steps(1, dict(gate=0, route=1, weigh=1, mask=4), {}, last=True)

        HEAD = ["ln", "norm", "turn", ("inproj", 0), ("inproj", 1), ("conv", 0), ("inproj", 2), ("conv", 1),
                ("inproj", 3), ("conv", 2), ("conv", 3), "gz", "u", "xproj", ("dtproj", 0), ("dtproj", 1),
                "exp", "log", "soft"]
        HEAD_AT = {0: [3.5, 3.5, 8, 8.5, 10, 10, 10, 10.5, 10.5, 10.5, 10.5, 12, 12, 14, 14.5, 15.5, 16.5, 17.5, 19.5],
                   1: [35.5, 35.5, 40.5, 42, 43, 43.5, 44, 45, 45.5, 45.5, 45.5, 47.5, 49, 51, 52.5, 54, 54, 55, 57]}
        STATES_AT = {0: [21.5, 24, 25.9, 28.8, 30.2, 33.6, 34.55, 37, 40.25, 42, 43.75, 46.2, 49.7, 51.8, 53.4, 54.25],
                     1: [59, 61.3, 62.45, 64.1, 65.75, 67.9, 69.55, 70.7, 71.85, 75, 76.75, 79.25, 81.25, 82.85, 85.8, 86.25]}
        END_AT = {0: [54.7, 59, 61], 1: [86.5, 92, 92]}
        B_AHEAD = 0.3

        def weave():
            mixers = [(at, ("M", name, n)) for n in range(2)
                      for names, places in ((HEAD, HEAD_AT[n]), (range(S), STATES_AT[n]), (("gather", "outproj", "epi"), END_AT[n]))
                      for name, at in zip(names, places, strict=True)]
            mixers += [(STATES_AT[n][st] - B_AHEAD, ("M", ("B", st + 1), n)) for n in range(2) for st in range(S - 1)]
            mixers.sort(key=lambda placed: placed[0])
            steps, units = [], 0
            for step in LOOP_F:
                if isinstance(step[1], int):
                    while mixers and mixers[0][0] <= units:
                        steps.append(mixers.pop(0)[1])
                    units += 1
                steps.append(step)
            return steps + [step for _, step in mixers]

        LOOP = weave()

        def behind(later, earlier):
            assert LOOP.index(later) > LOOP.index(earlier), (later, earlier)

        for n in range(2):
            order = HEAD + list(range(S)) + ["gather", "outproj", "epi"]
            for later, earlier in zip(order[1:], order):
                behind(("M", later, n), ("M", earlier, n))
            for st in range(S - 1):
                behind(("M", ("B", st + 1), n), ("M", st - 1 if st else "soft", n))
                behind(("M", st, n), ("M", ("B", st + 1), n))
        behind(("M", "ln", 1), ("M", 0, 0))
        behind(("M", "outproj", 0), ("M", ("dtproj", 1), 1))
        behind(("M", 0, 1), ("M", "outproj", 0))
        behind(("M", "soft", 1), ("M", S - 1, 0))
        behind(("M", "ln", 0), ("F", "epi", 0))
        behind(("M", "ln", 1), ("F", "epi", 1))
        behind(("F", "ln", 3), ("M", "epi", 0))
        behind(("F", "ln", 4), ("M", "epi", 1))
        LOOP_PASSES = 3

        def written(steps, upto=None):
            return sum(st[1] == "epi" for st in steps[:upto])

        def last_side(steps, upto=None):
            at = max(i for i, (kind, st, _) in enumerate(steps[:upto]) if kind == "F" and st in SIDE)
            return steps[at][1], sum(step[:2] == steps[at][:2] for step in steps[:at + 1]), written(steps, at + 1)

        SIDE = ("turn", "gate", "mask", "epi")
        assert last_side(FIRST)[0] == last_side(LOOP)[0]

        def run(step_f, step_m, fori):
            for i, (_, st, n) in enumerate(FIRST):
                side = last_side(FIRST, i) if st in SIDE and i > FIRST.index(("F", "turn", 0)) else None
                step_f(st, n, n, n % 3, written(FIRST, i), side)
            with fori(0, 2) as k:
                for i, (kind, st, n) in enumerate(LOOP):
                    w = None
                    if st in ("ln", "epi"):
                        w = k * written(LOOP) + (written(FIRST) + written(LOOP, i))
                    if kind == "F":
                        b = k * -1 + n if 1 <= n <= 3 else k * 3
                        side = None
                        if st in SIDE:
                            name, *counts = last_side(FIRST + LOOP, len(FIRST) + i)
                            _, *later = last_side(FIRST + LOOP + LOOP, len(FIRST) + len(LOOP) + i)
                            side = (name, *(k * (c1 - c0) + c0 for c0, c1 in zip(counts, later)))
                        step_f(st, k * LOOP_PASSES + n, b, n % 3, w, side)
                    else:
                        step_m(st, k * 2 + n, n, w)
            for i, (_, st, n) in enumerate(LAST):
                before = FIRST + LOOP + LOOP + LAST[:i]
                step_f(st, 2 * B - 2 + n, B - 2 + n, n % 3, written(before), last_side(before))

        def at_start(g):
            return isinstance(g, int) and g == 0

        block = ctx.enter_context(nc.Block())

        @block.sync
        def _(sp):
            xv = x.rearrange("b (t p) d -> b p t d", p=P)
            ov = out.rearrange("b (t p) d -> b p t d", p=P)
            sp.dma_start(xres[:, 0, :, :], xv[0]).then_inc(ld_x[0], 16)
            sp.dma_start(ident[:, :], ident_in).then_inc(ld_ident, 16)
            sp.dma_start(w1_stage[0], W1[0]).then_inc(ld_w1[0], 16)
            sp.dma_start(w_gate[:, :], W_gate).then_inc(ld_small, 16)
            sp.dma_start(vec_rows[0:UNITS, :], b1.rearrange("e (h p) -> (e h) p", p=P)).then_inc(ld_small, 16)
            for i, v in enumerate((conv_b, dt_proj_b, D_param)):
                sp.dma_start(vec_rows[UNITS + i * NH:UNITS + (i + 1) * NH, :],
                             v.rearrange("(h p) -> h p", p=P)).then_inc(ld_small, 16)
            sp.dma_start(vec_rows[UNITS + 3 * NH:, :], b2).then_inc(ld_small, 16)
            for e in range(E):
                if e > 0:
                    sp.dma_start(w1_stage[e], W1[e]).then_inc(ld_w1[e], 16)
                if e % 2 == 1:
                    sp.dma_start(w2[:, e - 1:e + 1, :, :],
                                 W2[e - 1:e + 1].rearrange("e (h p) d -> p e h d", p=P)).then_inc(ld_w2[e // 2], 16)
            for b in range(1, B):
                sp.dma_start(xres[:, b, :, :], xv[b]).then_inc(ld_x[b], 16)
            sp.dma_start(in_stage, in_proj_w).then_inc(ld_mix, 16)
            sp.dma_start(conv_sb[:, :, :], conv_w.rearrange("(h p) k -> p h k", p=P)).then_inc(ld_mix, 16)
            xpv = x_proj_w.rearrange("(h p) r -> p h r", p=P)
            sp.dma_start(xproj_sb[:, :, 0:2 * S], xpv[:, :, R:R + 2 * S]).then_inc(ld_mix, 16)
            sp.dma_start(xproj_sb[:, :, 2 * S:], xpv[:, :, 0:R]).then_inc(ld_mix, 16)
            sp.dma_start(dtw_sb[2 * S:, :], dt_proj_w).then_inc(ld_mix, 16)
            sp.dma_start(alog_sb[:, :, :], A_log.rearrange("(h p) s -> p h s", p=P)).then_inc(ld_mix, 16)
            sp.dma_start(outp_sb[:, :, :], out_proj_w.rearrange("(h p) d -> p h d", p=P)).then_inc(ld_mix, 16)

            def step_f(st, g, b, r, w, side):
                if st != "mask":
                    return
                sp.wait_ge(f_mcopied, g + 1)
                sp.dma_start(mask_dram[r], maskT[:, :]).then_inc(mask_out, 16)
                for c in range(E // 2):
                    if c == 0:
                        sp.wait_ge(mask_out, 16 * g + 16)
                    elif not at_start(g):
                        sp.wait_ge(f_scaled, E * g - (E - 2 * c - 2))
                    sp.dma_start(mask_bc[:, 2 * c:2 * c + 2, :].rearrange("p e t -> p (e t)"),
                                 mask_dram[r, 2 * c:2 * c + 2, :].rearrange("e t -> (e t)").partition_broadcast(P))\
                        .then_inc(mask_in[c], 16)

            run(step_f, lambda *_: None, sp.Fori)
            for b in range(B):
                total = written(FIRST) + 2 * written(LOOP) + written(LAST)
                sp.wait_ge(x_written, total if b == B - 1 else total - 1)
                sp.dma_start(ov[b], xres[:, b, :, :]).then_inc(stored, 16)
            sp.wait_ge(stored, 16 * B)

        @block.gpsimd
        def _(pool):
            nc.gpsimd.memset(neg_half[:, :], -0.5).then_inc(const_set, 1)
            nc.gpsimd.memset(xpad[:, :, 0:TAPS - 1], 0.0).then_inc(const_set, 1)
            pool.wait_ge(const_set, 2)

            def normalise(src, mv, var, rstd, norm, ln, power, normed, n):
                pool.wait_ge(ln, 3 * n + 3)
                nc.gpsimd.tensor_tensor(rstd[:, :], var[:, :], neg_half[:, :], ALU.pow).then_inc(power, 1)
                mean = mv[:, :, 0:1].to_broadcast([P, TT, D])
                nc.gpsimd.tensor_tensor(norm, src, mean, ALU.subtract).then_inc(power, 1)
                pool.wait_ge(power, 2 * n + 2)
                scale = rstd[:, :].unsqueeze(2).to_broadcast([P, TT, D])
                nc.gpsimd.tensor_tensor(norm, norm, scale, ALU.mult).then_inc(normed, 1)

            def step_f(st, g, b, r, w, side):
                if st == "norm":
                    normalise(xres[:, b, :, :], f_mv, f_var, f_rstd, f_norm[:, :, :], f_ln, f_pow, f_normed, g)
                if isinstance(st, tuple) and st[0] == "add":
                    add(g, st[1])

            def add(g, e):
                pool.wait_ge(f_scaled, E * g + e + 1)
                if e >= 2:
                    pool.wait_ge(f_added, (E - 1) * g + e - 1)
                nc.gpsimd.tensor_tensor(y_sum[:, :], y_sum[:, :], y_part[:, e % 2, :], ALU.add).then_inc(f_added, 1)

            def step_m(st, m, h2, w):
                if st == "norm":
                    normalise(xres[:, m, :, :], m_mv, m_var, m_rstd, m_norm[:, 0:TT, :], m_ln, m_pow, m_normed, m)
                if isinstance(st, int):
                    if st == 0:
                        pool.wait_ge(m_skip, m + 1)
                    else:
                        pool.wait_ge(m_sum, S * m + st)
                    pool.wait_ge(m_read, S * m + st + 1)
                    nc.gpsimd.tensor_tensor(y_ssm[:, :, :], y_ssm[:, :, :], read[:, st % 2, :, :], ALU.add)\
                        .then_inc(m_sum, 1)
                if st == "gz":
                    pool.wait_ge(m_th1, m + 1)
                    nc.gpsimd.tensor_tensor(zg[:, h2], zg[:, h2], z_th[:, :, :], ALU.mult).then_inc(m_gz, 1)
                if st == "gather":
                    pool.wait_ge(m_sum, S * m + S)
                    pool.wait_ge(m_gz, m + 1)
                    nc.gpsimd.tensor_tensor(y_ssm[:, :, :], y_ssm[:, :, :], zg[:, h2], ALU.mult).then_inc(m_y, 1)

            run(step_f, step_m, pool.Fori)

        @block.scalar
        def _(act):
            def w1_high(e):
                act.wait_ge(ld_w1[e], 16)
                nc.scalar.copy(w1_hi[:, e, :], w1_stage[e]).then_inc(w1_hi_done, 1)

            def mixer_weights():
                act.wait_ge(ld_mix, 112)
                nc.scalar.copy(in_hi[:, :], in_stage).then_inc(mix_exp, 1)
                nc.scalar.activation(aexp_sb[:, :, :], alog_sb[:, :, :], ACT.Exp).then_inc(mix_exp, 1)

            def step_f(st, g, b, r, w, side):
                if st == "turn":
                    if at_start(g):
                        w1_high(0)
                    act.wait_ge(f_turned, g + 1)
                    nc.scalar.copy(f_xT[:, :], fs_ps[:, :]).then_inc(f_copied, 1)
                if st == "split":
                    act.wait_ge(f_copied, g + 1)
                    nc.scalar.copy(f_xhi[:, :], f_xT[:, :]).then_inc(f_hi, 1)
                    if at_start(g):
                        act.wait_ge(vec_turned, 1)
                        nc.scalar.copy(vec_cols[:, :], ms_ps[:, 0:VECS]).then_inc(vec_ready, 1)
                        w1_high(1)
                if st == "route":
                    act.wait_ge(f_route, 8 * g + 3)
                    nc.scalar.activation(gexp[:, :, :], gshift[:, :, :], ACT.Exp).then_inc(f_exp, 1)
                if st == "mask":
                    act.wait_ge(f_mturned, g + 1)
                    if not at_start(g):
                        act.wait_ge(mask_out, 16 * g)
                    nc.scalar.copy(maskT[:, :], fs_ps[0:E, :]).then_inc(f_mcopied, 1)
                if isinstance(st, int):
                    if at_start(g) and st % HT == 0 and st // HT + 2 < E:
                        w1_high(st // HT + 2)
                    if at_start(g) and st == 5 * HT + 2:
                        mixer_weights()
                    if at_start(g) and st == 0:
                        act.wait_ge(vec_ready, 1)
                    act.wait_ge(f_up, UNITS * g + st + 1)
                    if not (at_start(g) and st < NHB):
                        act.wait_ge(f_down, UNITS * g + st - NHB + 1)
                    nc.scalar.activation(hid[:, st % NHB, :], z_ps[st % 2][:, :], ACT.Relu,
                                         bias=vec_cols[:, st:st + 1]).then_inc(f_relu, 1)

            def decays(m, s):
                if s == 0:
                    act.wait_ge(m_dt, m + 1)
                if not (isinstance(m, int) and m == 0 and s < 2):
                    if s >= 2:
                        act.wait_ge(m_scan, NH * (S * m + s - 1))
                for h in range(NH):
                    nc.scalar.activation(decay[:, s % 2, h, :], dt[:, h, :], ACT.Exp,
                                         scale=a_neg[:, h, s:s + 1]).then_inc(m_decay, 1)

            def step_m(st, m, h2, w):
                if st == "turn":
                    act.wait_ge(m_turned, m + 1)
                    nc.scalar.copy(m_xhi[:, :], ms_ps[:, :]).then_inc(m_hi, 1)
                if isinstance(st, tuple) and st[0] == "inproj":
                    j = st[1]
                    act.wait_ge(m_inproj, 2 * NH * m + j + 1)
                    if j < NH:
                        nc.scalar.copy(xpad[:, j, TAPS - 1:], ms_ps[:, :]).then_inc(m_evac, 1)
                    else:
                        nc.scalar.copy(zg[:, h2, j - NH, :], ms_ps[:, :])
                        nc.scalar.activation(z_th[:, j - NH, :], ms_ps[:, :], ACT.Tanh, scale=0.5).then_inc(m_evac, 1)
                if st == ("conv", 0):
                    act.wait_ge(m_evac, 2 * NH * m + NH)
                    act.wait_ge(const_set, 2)
                    act.wait_ge(mix_prep, 4)
                    for h in range(NH):
                        nc.scalar.activation(conv[:, h, :], xpad[:, h, 0:T], ACT.Identity, scale=conv_half[:, h, 0:1],
                                             bias=convb_half[:, h:h + 1]).then_inc(m_tap0, 1)
                if st == "gz":
                    act.wait_ge(m_evac, 2 * NH * m + 2 * NH)
                    nc.scalar.activation(z_th[:, :, :], z_th[:, :, :], ACT.Identity, bias=1.0).then_inc(m_th1, 1)
                if st == "u":
                    act.wait_ge(m_conv, NH * (TAPS - 1) * (m + 1))
                    nc.scalar.activation(conv_th[:, :, :], conv[:, :, :], ACT.Tanh).then_inc(m_tanh, 1)
                if st == "xproj":
                    act.wait_ge(m_xproj, m + 1)
                    nc.scalar.copy(bc[0:2 * S, h2, :], ms_ps[0:2 * S, :]).then_inc(m_bchi, 1)
                    nc.scalar.copy(dt_low[2 * S:, :], ms_ps[2 * S:2 * S + R, :]).then_inc(m_bchi, 1)
                if isinstance(st, tuple) and st[0] == "dtproj":
                    h = st[1]
                    act.wait_ge(m_dtproj, NH * m + h + 1)
                    nc.scalar.activation(dt_lin[:, h, :], ms_ps[:, :], ACT.Identity, bias=dtb_sb[:, h:h + 1])
                    nc.scalar.activation(dt_abs[:, h, :], ms_ps[:, :], ACT.Abs, bias=dtb_sb[:, h:h + 1])\
                        .then_inc(m_soft, 1)
                if st == "exp":
                    act.wait_ge(m_soft, 4 * m + 2)
                    nc.scalar.activation(dt_abs[:, :, :], dt_abs[:, :, :], ACT.Exp, scale=-1.0).then_inc(m_soft, 1)
                if st == "log":
                    act.wait_ge(m_soft, 4 * m + 3)
                    nc.scalar.activation(dt_abs[:, :, :], dt_abs[:, :, :], ACT.Ln, bias=1.0).then_inc(m_soft, 1)
                if st == "soft":
                    decays(m, 0)
                if st == 0:
                    if h2 == 1:
                        act.wait_ge(m_outproj, m)
                    for h in range(NH):
                        ins = nc.scalar.activation(y_ssm[:, h, :], u[:, h, :], ACT.Copy, scale=dskip_sb[:, h:h + 1])
                    ins.then_inc(m_skip, 1)
                if isinstance(st, int) and st + 1 < S:
                    decays(m, st + 1)

            run(step_f, step_m, act.Fori)

        @block.tensor
        def _(pe):
            def side_free(side):
                name, n, writes = side
                if name == "turn":
                    pe.wait_ge(f_copied, n)
                if name == "gate":
                    pe.wait_ge(f_route, 8 * n - 7)
                if name == "mask":
                    pe.wait_ge(f_mcopied, n)
                if name == "epi":
                    pe.wait_ge(x_written, writes)

            def down(g, i):
                e, ht = i // HT, i % HT
                pe.wait_ge(f_relu, UNITS * g + i + 1)
                if ht == 0 and not (at_start(g) and e < 2):
                    pe.wait_ge(f_scaled, E * g + e - 1)
                if at_start(g) and ht == 0 and e % 2 == 0:
                    pe.wait_ge(ld_w2[e // 2], 16)
                nc.tensor.matmul(ye_ps[e % 2][:, :], w2[:, e, ht, :], hid[:, i % NHB, :],
                                 start=(ht == 0), stop=(ht == HT - 1)).then_inc(f_down, 1)

            def step_f(st, g, b, r, w, side):
                if st == "turn":
                    pe.wait_ge(f_normed, g + 1)
                    if at_start(g):
                        pe.wait_ge(ld_ident, 16)
                    else:
                        side_free(side)
                    for t in range(TT):
                        mm = nc.tensor.transpose(fs_ps[:, t * P:(t + 1) * P], f_norm[:, t, :], ident[:, :])
                    mm.then_inc(f_turned, 1)
                    if at_start(g):
                        pe.wait_ge(ld_small, 96)
                        nc.tensor.transpose(ms_ps[:, 0:VECS], vec_rows[:, :], ident[0:VECS, 0:VECS]).then_inc(vec_turned, 1)
                if st == "gate":
                    pe.wait_ge(f_copied, g + 1)
                    side_free(side)
                    for t in range(TT):
                        mm = nc.tensor.matmul(fs_ps[:, t * E:(t + 1) * E], f_xT[:, t * P:(t + 1) * P], w_gate[:, :],
                                              start=True, stop=True)
                    mm.then_inc(f_gated, 1)
                if st == "mask":
                    pe.wait_ge(f_route, 8 * g + 8)
                    side_free(side)
                    for t in range(TT):
                        mm = nc.tensor.transpose(fs_ps[0:E, t * P:(t + 1) * P], mask[:, t, :], ident[:, :])
                    mm.then_inc(f_mturned, 1)
                if isinstance(st, int):
                    e = st // HT
                    if st == 0:
                        pe.wait_ge(f_hi, g + 1)
                    if at_start(g) and st % HT == 0:
                        pe.wait_ge(w1_lo_done, e + 1)
                    if not (at_start(g) and st < 2):
                        pe.wait_ge(f_relu, UNITS * g + st - 1)
                    cols = slice((st % HT) * P, (st % HT + 1) * P)
                    for i, (w, v) in enumerate(((w1_hi, f_xhi), (w1_lo, f_xhi), (w1_hi, f_xlo))):
                        if st == 0 and i == 2:
                            pe.wait_ge(f_lo, g + 1)
                        mm = nc.tensor.matmul(z_ps[st % 2][:, :], w[:, e, cols], v[:, :], start=(i == 0), stop=(i == 2))
                    mm.then_inc(f_up, 1)
                    if st >= 2:
                        down(g, st - 2)
                if st == "tail":
                    down(g, UNITS - 2)
                    down(g, UNITS - 1)
                if st == "epi":
                    pe.wait_ge(f_added, (E - 1) * g + E - 1)
                    side_free(side)
                    for t in range(TT):
                        cols = slice(t * P, (t + 1) * P)
                        mm = nc.tensor.transpose(fs_ps[:, cols], y_sum[:, cols], ident[:, :])
                    mm.then_inc(f_back, 1)

            def spread_row(ps, j, h2):
                return nc.tensor.matmul(ps[:, :], spread[:, j, :], bc[:, h2, :], start=True, stop=True)

            def step_m(st, m, h2, w):
                if st == "turn":
                    pe.wait_ge(m_normed, m + 1)
                    for t in range(TT):
                        mm = nc.tensor.transpose(ms_ps[:, t * P:(t + 1) * P], m_norm[:, t, :], ident[:, :])
                    mm.then_inc(m_turned, 1)
                if isinstance(st, tuple) and st[0] == "inproj":
                    j = st[1]
                    if j == 0:
                        pe.wait_ge(m_lo, m + 1)
                        pe.wait_ge(mix_split, 1)
                    else:
                        pe.wait_ge(m_evac, 2 * NH * m + j)
                    cols = slice(j * P, (j + 1) * P)
                    for i, (w_, v) in enumerate(((in_hi, m_xhi), (in_hi, m_xlo), (in_lo, m_xhi))):
                        mm = nc.tensor.matmul(ms_ps[:, :], w_[:, cols], v[:, :], start=(i == 0), stop=(i == 2))
                    mm.then_inc(m_inproj, 1)
                if st == "xproj":
                    pe.wait_ge(m_u, m + 1)
                    pe.wait_ge(m_evac, 2 * NH * m + 4)
                    for h in range(NH):
                        mm = nc.tensor.matmul(ms_ps[0:2 * S + R, :], xproj_sb[:, h, :], u[:, h, :],
                                              start=(h == 0), stop=(h == NH - 1))
                    mm.then_inc(m_xproj, 1)
                if isinstance(st, tuple) and st[0] == "dtproj":
                    h = st[1]
                    if h == 0:
                        pe.wait_ge(m_bchi, 2 * m + 2)
                        pe.wait_ge(m_bclo, m + 1)
                    else:
                        pe.wait_ge(m_soft, 4 * m + h)
                    nc.tensor.matmul(ms_ps[:, :], dtw_sb[2 * S:, h * P:(h + 1) * P], dt_low[2 * S:, :],
                                     start=True, stop=True).then_inc(m_dtproj, 1)
                if st == "soft":
                    if h2 == 1:
                        pe.wait_ge(m_inject, S * m)
                    pe.wait_ge(spread_set, 4)
                    spread_row(b_ps, 0, h2).then_inc(m_B, 1)
                if isinstance(st, int):
                    if st >= 1 or h2 == 1:
                        pe.wait_ge(m_read, S * m + st)
                    spread_row(c_ps, S + st, h2).then_inc(m_C, 1)
                if isinstance(st, tuple) and st[0] == "B":
                    pe.wait_ge(m_inject, S * m + st[1])
                    spread_row(b_ps, st[1], h2).then_inc(m_B, 1)
                if st == "outproj":
                    pe.wait_ge(m_y, m + 1)
                    if h2 == 0:
                        pe.wait_ge(m_soft, 4 * m + 6)
                    for t in range(TT):
                        cols = slice(t * P, (t + 1) * P)
                        for h in range(NH):
                            mm = nc.tensor.matmul(ms_ps[:, cols], y_ssm[:, h, cols], outp_half[:, h, :],
                                                  start=(h == 0), stop=(h == NH - 1))
                    mm.then_inc(m_outproj, 1)

            run(step_f, step_m, pe.Fori)

        @block.vector
        def _(dve):
            def make_spread(c):
                r, j = c // 2 * 2 * S, c % 2 * S
                src = ident[r:r + 2 * S, r + j:r + j + S].unsqueeze(2).to_broadcast([2 * S, S, P])
                nc.vector.tensor_copy(spread[r:r + 2 * S, j:j + S, :], src).then_inc(spread_set, 1)

            def w1_low(e):
                dve.wait_ge(w1_hi_done, e + 1)
                nc.vector.tensor_tensor(w1_lo[:, e, :], w1_stage[e], w1_hi[:, e, :].bitcast(f32), ALU.subtract)\
                    .then_inc(w1_lo_done, 1)

            def mixer_weights():
                dve.wait_ge(mix_exp, 2)
                nc.vector.tensor_tensor(in_lo[:, :], in_stage, in_hi[:, :].bitcast(f32), ALU.subtract).then_inc(mix_split, 1)
                nc.vector.tensor_scalar(a_neg[:, :, :], aexp_sb[:, :, :], -1.0, None, ALU.mult).then_inc(mix_prep, 1)
                nc.vector.tensor_scalar(conv_half[:, :, :], conv_sb[:, :, :], 0.5, None, ALU.mult).then_inc(mix_prep, 1)
                nc.vector.tensor_scalar(convb_half[:, :], convb_sb[:, :], 0.5, None, ALU.mult).then_inc(mix_prep, 1)
                nc.vector.tensor_scalar(outp_half[:, :, :], outp_sb[:, :, :], 0.5, None, ALU.mult).then_inc(mix_prep, 1)
                dve.wait_ge(mix_prep, 4)

            def variance(src, stat, mv, var, ln, n):
                nc.vector.memset(unused[:, :], 0.0)
                for t in range(TT):
                    ins = nc.vector.bn_stats(stat[:, t, :], src(t))
                ins.then_inc(ln, 1)
                dve.wait_ge(ln, 3 * n + 1)
                nc.vector.memset(unused[:, :], 0.0)
                for t in range(TT):
                    ins = nc.vector.bn_aggr(mv[:, t, :], stat[:, t, :])
                ins.then_inc(ln, 1)
                dve.wait_ge(ln, 3 * n + 2)
                nc.vector.tensor_scalar(var[:, :], mv[:, :, 1], EPS, None, ALU.add).then_inc(ln, 1)

            def per_token(v, j):
                return v[:, :, j:j + 1].to_broadcast([P, TT, E])

            def scale(g, e):
                dve.wait_ge(f_down, UNITS * g + HT * (e + 1))
                if e % 2 == 0:
                    dve.wait_ge(mask_in[e // 2], 16 * g + 16)
                if e >= 3:
                    dve.wait_ge(f_added, (E - 1) * g + e - 2)
                dst = y_sum[:, :] if e == 0 else y_part[:, e % 2, :]
                nc.vector.scalar_tensor_tensor(out=dst, in0=ye_ps[e % 2][:, :], scalar=b2_cols[:, e:e + 1],
                                               in1=mask_bc[:, e, :], op0=ALU.add, op1=ALU.mult).then_inc(f_scaled, 1)

            def step_f(st, g, b, r, w, side):
                if st == "ln":
                    if isinstance(g, int) and g < B:
                        dve.wait_ge(ld_x[g], 16)
                        if g == 1:
                            for later in ld_x[2:]:
                                dve.wait_ge(later, 16)
                    if not at_start(g):
                        dve.wait_ge(x_written, w)
                    variance(lambda t: xres[:, b, t, :], f_stat, f_mv, f_var, f_ln, g)
                if st == "split":
                    dve.wait_ge(f_hi, g + 1)
                    nc.vector.tensor_tensor(f_xlo[:, :], f_xT[:, :], f_xhi[:, :].bitcast(f32), ALU.subtract)\
                        .then_inc(f_lo, 1)
                    if at_start(g):
                        w1_low(1)
                if st == "turn" and at_start(g):
                    w1_low(0)
                if st == "route":
                    q = 8 * g
                    dve.wait_ge(f_gated, g + 1)
                    nc.vector.tensor_copy(gate[:, :, :], fs_ps[:, 0:TT * E].rearrange("p (t e) -> p t e", e=E))\
                        .then_inc(f_route, 1)
                    dve.wait_ge(f_route, q + 1)
                    nc.vector.memset(unused[:, :], 0.0)
                    for t in range(TT):
                        ins = nc.vector.max(top[:, t, :], gate[:, t, :])
                    ins.then_inc(f_route, 1)
                    dve.wait_ge(f_route, q + 2)
                    nc.vector.tensor_tensor(gshift[:, :, :], gate[:, :, :], per_token(top, 0), ALU.subtract).then_inc(f_route, 1)
                    nc.vector.tensor_tensor(gkeep[:, :, :], gate[:, :, :], per_token(top, 1), ALU.is_ge).then_inc(f_route, 1)
                if st == "weigh":
                    q = 8 * g
                    dve.wait_ge(f_route, q + 4)
                    dve.wait_ge(f_exp, g + 1)
                    nc.vector.tensor_tensor(gexp[:, :, :], gexp[:, :, :], gkeep[:, :, :], ALU.mult).then_inc(f_route, 1)
                    dve.wait_ge(f_route, q + 5)
                    nc.vector.tensor_reduce(gsum[:, :], gexp[:, :, :], AX.X, ALU.add).then_inc(f_route, 1)
                    dve.wait_ge(f_route, q + 6)
                    nc.vector.reciprocal(grec[:, :], gsum[:, :]).then_inc(f_route, 1)
                    dve.wait_ge(f_route, q + 7)
                    nc.vector.scalar_tensor_tensor(out=mask[:, :, :], in0=gexp[:, :, :], scalar=FFN_SCALE,
                                                   in1=grec[:, :].unsqueeze(2).to_broadcast([P, TT, E]),
                                                   op0=ALU.mult, op1=ALU.mult).then_inc(f_route, 1)
                if at_start(g) and isinstance(st, int) and st % HT == 0 and st // HT + 2 < E:
                    w1_low(st // HT + 2)
                if at_start(g) and isinstance(st, int) and st % HT == 1 and 2 <= st // HT < 6:
                    if st // HT == 2:
                        dve.wait_ge(ld_ident, 16)
                    make_spread(st // HT - 2)
                if at_start(g) and st == 5 * HT + 2:
                    mixer_weights()
                if isinstance(st, tuple) and st[0] == "scale":
                    scale(g, st[1])
                if st == "epi":
                    dve.wait_ge(f_back, g + 1)
                    dve.wait_ge(x_written, w)
                    xb = xres[:, b, :, :].rearrange("p t d -> p (t d)")
                    nc.vector.tensor_tensor(xb, fs_ps[:, :], xb, ALU.add).then_inc(x_written, 1)

            def halves(ps):
                return ps[:, :].unsqueeze(1).to_broadcast([P, NH, T])

            def inject_step(m, s):
                dve.wait_ge(m_B, S * m + s + 1)
                nc.vector.tensor_tensor(inject[:, s % 2, :, :], dtu[:, :, :], halves(b_ps), ALU.mult).then_inc(m_inject, 1)

            def step_m(st, m, h2, w):
                if st == "ln":
                    dve.wait_ge(x_written, w)
                    variance(lambda t: xres[:, m, t, :], m_stat, m_mv, m_var, m_ln, m)
                if st == "turn":
                    dve.wait_ge(m_hi, m + 1)
                    nc.vector.tensor_tensor(m_xlo[:, :], ms_ps[:, :], m_xhi[:, :].bitcast(f32), ALU.subtract)\
                        .then_inc(m_lo, 1)
                if isinstance(st, tuple) and st[0] == "conv":
                    k = st[1]
                    for h in range(NH if k else 0):
                        if k == 1:
                            dve.wait_ge(m_tap0, NH * m + h + 1)
                        else:
                            dve.wait_ge(m_conv, NH * (TAPS - 1) * m + NH * (k - 2) + h + 1)
                        nc.vector.scalar_tensor_tensor(out=conv[:, h, :], in0=xpad[:, h, k:k + T],
                                                       scalar=conv_half[:, h, k:k + 1], in1=conv[:, h, :],
                                                       op0=ALU.mult, op1=ALU.add).then_inc(m_conv, 1)
                if st == "u":
                    dve.wait_ge(m_tanh, m + 1)
                    nc.vector.scalar_tensor_tensor(out=u[:, :, :], in0=conv_th[:, :, :], scalar=1.0, in1=conv[:, :, :],
                                                   op0=ALU.add, op1=ALU.mult).then_inc(m_u, 1)
                if st == "xproj":
                    dve.wait_ge(m_bchi, 2 * m + 1)
                    nc.vector.tensor_tensor(bc[2 * S:4 * S, h2, :], ms_ps[0:2 * S, :], bc[0:2 * S, h2, :].bitcast(f32), ALU.subtract)\
                        .then_inc(m_bclo, 1)
                if st == "soft":
                    dve.wait_ge(m_soft, 4 * m + 4)
                    nc.vector.scalar_tensor_tensor(out=dt[:, :, :], in0=dt_lin[:, :, :], scalar=0.0, in1=dt_abs[:, :, :],
                                                   op0=ALU.max, op1=ALU.add).then_inc(m_dt, 1)
                    dve.wait_ge(m_dt, m + 1)
                    dve.wait_ge(m_u, m + 1)
                    nc.vector.tensor_tensor(dtu[:, :, :], dt[:, :, :], u[:, :, :], ALU.mult).then_inc(m_dtu, 1)
                    dve.wait_ge(m_dtu, m + 1)
                    inject_step(m, 0)
                if isinstance(st, int):
                    n = S * m + st
                    dve.wait_ge(m_inject, n + 1)
                    for h in range(NH):
                        dve.wait_ge(m_decay, NH * n + h + 1)
                        nc.vector.tensor_tensor_scan(state[:, st % 2, h, :], decay[:, st % 2, h, :],
                                                     inject[:, st % 2, h, :], 0.0, ALU.mult, ALU.add).then_inc(m_scan, 1)
                    if st + 1 < S:
                        inject_step(m, st + 1)
                    dve.wait_ge(m_scan, NH * n + NH)
                    dve.wait_ge(m_C, n + 1)
                    if st >= 2 or h2 == 1:
                        dve.wait_ge(m_sum, S * m + st - 1)
                    nc.vector.tensor_tensor(read[:, st % 2, :, :], state[:, st % 2, :, :], halves(c_ps), ALU.mult).then_inc(m_read, 1)
                if st == "epi":
                    dve.wait_ge(m_outproj, m + 1)
                    dve.wait_ge(x_written, w)
                    xb = xres[:, m, :, :].rearrange("p t d -> p (t d)")
                    nc.vector.tensor_tensor(xb, ms_ps[:, :], xb, ALU.add).then_inc(x_written, 1)

            run(step_f, step_m, dve.Fori)


_INS = ["L0_attn_x", "L0_attn_in_proj_w", "L0_attn_conv_w", "L0_attn_conv_b", "L0_attn_x_proj_w",
        "L0_attn_dt_proj_w", "L0_attn_dt_proj_b", "L0_attn_A_log", "L0_attn_D_param", "L0_attn_out_proj_w",
        "L0_ffn_W_gate", "L0_ffn_W1", "L0_ffn_b1", "L0_ffn_W2", "L0_ffn_b2"]


def kernel(**inputs):
    import numpy as _np
    import concourse.bacc as _bacc
    from concourse import mybir as _mybir
    from concourse.bass_utils import run_bass_kernel_spmd as _run

    nc = _bacc.Bacc("TRN2", target_bir_lowering=False, num_devices=1)
    arrays, args = {}, []
    for name in _INS:
        a = _np.ascontiguousarray(inputs[name])
        arrays[f"in_{name}_dram"] = a
        args.append(nc.dram_tensor(f"in_{name}_dram", a.shape, _mybir.dt.from_np(a.dtype), kind="ExternalInput").ap())
    ident = _np.eye(128, dtype=_np.float32)
    arrays["in_ident_dram"] = ident
    args.append(nc.dram_tensor("in_ident_dram", ident.shape, _mybir.dt.float32, kind="ExternalInput").ap())
    shape = tuple(inputs["L0_attn_x"].shape)
    args.append(nc.dram_tensor("out_0_dram", shape, _mybir.dt.float32, kind="ExternalOutput").ap())
    macaron_kernel(nc, *args)
    r = _run(nc, [arrays], core_ids=[0])
    return r.results[0]["out_0_dram"]
```
